# Optimizing a Trainium2 kernel written in Bass

```python
import numpy as np
import jax
import jax.numpy as jnp

def _softmax(x, axis=-1):
    return jax.nn.softmax(x, axis=axis)

def _gelu(x):
    return jax.nn.gelu(x, approximate=True)

def _silu(x):
    return jax.nn.silu(x)

def _sigmoid(x):
    return jax.nn.sigmoid(x)

def _layernorm(x, axis=-1, eps=1e-05):
    m = jnp.mean(x, axis=axis, keepdims=True)
    v = jnp.var(x, axis=axis, keepdims=True)
    return (x - m) / jnp.sqrt(v + eps)

def _scatter_add(tgt, idx, src, axis=0):
    return tgt.at[idx].add(src)

def _segment_sum(src, seg, n):
    return jax.ops.segment_sum(src, seg, n)
kernel_name = 'mk_dlrm_tower_d1_rec_r8_6a1820'

def setup_inputs(seed: int=0):
    np.random.seed(seed)
    _w = jnp.asarray

    def _rec_inputs():
        import jax
        import jax.numpy as jnp
        _tk = jax.random.key(seed)
        dense_ctx = jax.random.normal(jax.random.fold_in(_tk, 190), (512, 16), jnp.float32)
        ids = jnp.stack([jax.random.randint(jax.random.fold_in(_tk, 200 + f), (512,), 0, v, jnp.int32) for f, v in enumerate([125000, 12500, 125000, 12500, 125000, 1000, 1000, 12500, 1250, 125000, 1250, 1250, 1250, 1000, 125000, 1250, 125000, 125000, 1250, 12500, 1000, 1250, 1250, 12500, 12500, 1250, 1000, 1000, 12500, 1000, 1250, 1000])], axis=1)
        tbl_0 = 0.05 * jax.random.normal(jax.random.fold_in(_tk, 500 + 0), (125000, 32), jnp.float32)
        tbl_1 = 0.05 * jax.random.normal(jax.random.fold_in(_tk, 500 + 1), (12500, 32), jnp.float32)
        tbl_2 = 0.05 * jax.random.normal(jax.random.fold_in(_tk, 500 + 2), (125000, 32), jnp.float32)
        tbl_3 = 0.05 * jax.random.normal(jax.random.fold_in(_tk, 500 + 3), (12500, 32), jnp.float32)
        tbl_4 = 0.05 * jax.random.normal(jax.random.fold_in(_tk, 500 + 4), (125000, 32), jnp.float32)
        tbl_5 = 0.05 * jax.random.normal(jax.random.fold_in(_tk, 500 + 5), (1000, 32), jnp.float32)
        tbl_6 = 0.05 * jax.random.normal(jax.random.fold_in(_tk, 500 + 6), (1000, 32), jnp.float32)
        tbl_7 = 0.05 * jax.random.normal(jax.random.fold_in(_tk, 500 + 7), (12500, 32), jnp.float32)
        tbl_8 = 0.05 * jax.random.normal(jax.random.fold_in(_tk, 500 + 8), (1250, 32), jnp.float32)
        tbl_9 = 0.05 * jax.random.normal(jax.random.fold_in(_tk, 500 + 9), (125000, 32), jnp.float32)
        tbl_10 = 0.05 * jax.random.normal(jax.random.fold_in(_tk, 500 + 10), (1250, 32), jnp.float32)
        tbl_11 = 0.05 * jax.random.normal(jax.random.fold_in(_tk, 500 + 11), (1250, 32), jnp.float32)
        tbl_12 = 0.05 * jax.random.normal(jax.random.fold_in(_tk, 500 + 12), (1250, 32), jnp.float32)
        tbl_13 = 0.05 * jax.random.normal(jax.random.fold_in(_tk, 500 + 13), (1000, 32), jnp.float32)
        tbl_14 = 0.05 * jax.random.normal(jax.random.fold_in(_tk, 500 + 14), (125000, 32), jnp.float32)
        tbl_15 = 0.05 * jax.random.normal(jax.random.fold_in(_tk, 500 + 15), (1250, 32), jnp.float32)
        tbl_16 = 0.05 * jax.random.normal(jax.random.fold_in(_tk, 500 + 16), (125000, 32), jnp.float32)
        tbl_17 = 0.05 * jax.random.normal(jax.random.fold_in(_tk, 500 + 17), (125000, 32), jnp.float32)
        tbl_18 = 0.05 * jax.random.normal(jax.random.fold_in(_tk, 500 + 18), (1250, 32), jnp.float32)
        tbl_19 = 0.05 * jax.random.normal(jax.random.fold_in(_tk, 500 + 19), (12500, 32), jnp.float32)
        tbl_20 = 0.05 * jax.random.normal(jax.random.fold_in(_tk, 500 + 20), (1000, 32), jnp.float32)
        tbl_21 = 0.05 * jax.random.normal(jax.random.fold_in(_tk, 500 + 21), (1250, 32), jnp.float32)
        tbl_22 = 0.05 * jax.random.normal(jax.random.fold_in(_tk, 500 + 22), (1250, 32), jnp.float32)
        tbl_23 = 0.05 * jax.random.normal(jax.random.fold_in(_tk, 500 + 23), (12500, 32), jnp.float32)
        tbl_24 = 0.05 * jax.random.normal(jax.random.fold_in(_tk, 500 + 24), (12500, 32), jnp.float32)
        tbl_25 = 0.05 * jax.random.normal(jax.random.fold_in(_tk, 500 + 25), (1250, 32), jnp.float32)
        tbl_26 = 0.05 * jax.random.normal(jax.random.fold_in(_tk, 500 + 26), (1000, 32), jnp.float32)
        tbl_27 = 0.05 * jax.random.normal(jax.random.fold_in(_tk, 500 + 27), (1000, 32), jnp.float32)
        tbl_28 = 0.05 * jax.random.normal(jax.random.fold_in(_tk, 500 + 28), (12500, 32), jnp.float32)
        tbl_29 = 0.05 * jax.random.normal(jax.random.fold_in(_tk, 500 + 29), (1000, 32), jnp.float32)
        tbl_30 = 0.05 * jax.random.normal(jax.random.fold_in(_tk, 500 + 30), (1250, 32), jnp.float32)
        tbl_31 = 0.05 * jax.random.normal(jax.random.fold_in(_tk, 500 + 31), (1000, 32), jnp.float32)
        _rk = jax.random.fold_in(_tk, 7)
        W_top1 = 0.0606339 * jax.random.normal(jax.random.fold_in(_tk, 801), (272, 512), jnp.float32)
        W_top2 = 0.0441942 * jax.random.normal(jax.random.fold_in(_tk, 802), (512, 256), jnp.float32)
        W_top3 = 0.0625 * jax.random.normal(jax.random.fold_in(_tk, 803), (256, 1), jnp.float32)
        b_top1 = jnp.zeros((512,), jnp.float32)
        b_top2 = jnp.zeros((256,), jnp.float32)
        return (dense_ctx, ids, tbl_0, tbl_1, tbl_2, tbl_3, tbl_4, tbl_5, tbl_6, tbl_7, tbl_8, tbl_9, tbl_10, tbl_11, tbl_12, tbl_13, tbl_14, tbl_15, tbl_16, tbl_17, tbl_18, tbl_19, tbl_20, tbl_21, tbl_22, tbl_23, tbl_24, tbl_25, tbl_26, tbl_27, tbl_28, tbl_29, tbl_30, tbl_31, W_top1, b_top1, W_top2, b_top2, W_top3)
    dense_ctx, ids, tbl_0, tbl_1, tbl_2, tbl_3, tbl_4, tbl_5, tbl_6, tbl_7, tbl_8, tbl_9, tbl_10, tbl_11, tbl_12, tbl_13, tbl_14, tbl_15, tbl_16, tbl_17, tbl_18, tbl_19, tbl_20, tbl_21, tbl_22, tbl_23, tbl_24, tbl_25, tbl_26, tbl_27, tbl_28, tbl_29, tbl_30, tbl_31, W_top1, b_top1, W_top2, b_top2, W_top3 = _rec_inputs()

    def _L0_rec_setup():
        import jax, jax.numpy as jnp
        import numpy as np
        B, F, D = (512, 32, 32)
        LAYER_SIZE = [128, 128]

        def _cin_forward(inputs, filters):
            x0 = inputs
            prev = inputs
            outs = []
            for W in filters:
                z = jnp.einsum('bhd,bmd->bhmd', x0, prev)
                b, h, m, d = z.shape
                z = z.reshape(b, h * m, d)
                cur = jnp.einsum('bpd,pn->bnd', z, W[0])
                cur = jax.nn.relu(cur)
                prev = cur
                outs.append(cur)
            result = jnp.concatenate(outs, axis=1)
            return jnp.sum(result, axis=-1)
        key = jax.random.key(seed)
        k1, k2, k3 = jax.random.split(key, 3)
        inputs = jax.random.normal(k1, (B, F, D), dtype=jnp.float32)
        field_nums = [F] + LAYER_SIZE
        filter_0 = jax.random.normal(k2, (1, field_nums[0] * field_nums[0], field_nums[1]), dtype=jnp.float32) * 0.05
        filter_1 = jax.random.normal(k3, (1, field_nums[0] * field_nums[1], field_nums[2]), dtype=jnp.float32) * 0.05
        return {'inputs': inputs, 'filter_0': filter_0, 'filter_1': filter_1}
    _L0_rec_all = _L0_rec_setup()
    _L0_rec_in = {k: v for k, v in _L0_rec_all.items() if k in ('filter_0', 'filter_1')}
    del _L0_rec_all
    return {'dense_ctx': dense_ctx, 'ids': ids, 'tbl_0': tbl_0, 'tbl_1': tbl_1, 'tbl_2': tbl_2, 'tbl_3': tbl_3, 'tbl_4': tbl_4, 'tbl_5': tbl_5, 'tbl_6': tbl_6, 'tbl_7': tbl_7, 'tbl_8': tbl_8, 'tbl_9': tbl_9, 'tbl_10': tbl_10, 'tbl_11': tbl_11, 'tbl_12': tbl_12, 'tbl_13': tbl_13, 'tbl_14': tbl_14, 'tbl_15': tbl_15, 'tbl_16': tbl_16, 'tbl_17': tbl_17, 'tbl_18': tbl_18, 'tbl_19': tbl_19, 'tbl_20': tbl_20, 'tbl_21': tbl_21, 'tbl_22': tbl_22, 'tbl_23': tbl_23, 'tbl_24': tbl_24, 'tbl_25': tbl_25, 'tbl_26': tbl_26, 'tbl_27': tbl_27, 'tbl_28': tbl_28, 'tbl_29': tbl_29, 'tbl_30': tbl_30, 'tbl_31': tbl_31, 'W_top1': W_top1, 'b_top1': b_top1, 'W_top2': W_top2, 'b_top2': b_top2, 'W_top3': W_top3, 'L0_rec_filter_0': _L0_rec_in['filter_0'], 'L0_rec_filter_1': _L0_rec_in['filter_1']}

def reference(dense_ctx, ids, tbl_0, tbl_1, tbl_2, tbl_3, tbl_4, tbl_5, tbl_6, tbl_7, tbl_8, tbl_9, tbl_10, tbl_11, tbl_12, tbl_13, tbl_14, tbl_15, tbl_16, tbl_17, tbl_18, tbl_19, tbl_20, tbl_21, tbl_22, tbl_23, tbl_24, tbl_25, tbl_26, tbl_27, tbl_28, tbl_29, tbl_30, tbl_31, W_top1, b_top1, W_top2, b_top2, W_top3, L0_rec_filter_0, L0_rec_filter_1):
    import jax
    import jax.numpy as jnp

    def _L0_rec_ref(inputs, filter_0, filter_1):
        import jax, jax.numpy as jnp
        import numpy as np
        B, F, D = (512, 32, 32)
        LAYER_SIZE = [128, 128]

        def _cin_forward(inputs, filters):
            x0 = inputs
            prev = inputs
            outs = []
            for W in filters:
                z = jnp.einsum('bhd,bmd->bhmd', x0, prev)
                b, h, m, d = z.shape
                z = z.reshape(b, h * m, d)
                cur = jnp.einsum('bpd,pn->bnd', z, W[0])
                cur = jax.nn.relu(cur)
                prev = cur
                outs.append(cur)
            result = jnp.concatenate(outs, axis=1)
            return jnp.sum(result, axis=-1)
        return _cin_forward(inputs, (filter_0, filter_1))
    e = jnp.stack([tbl_0[ids[:, 0]], tbl_1[ids[:, 1]], tbl_2[ids[:, 2]], tbl_3[ids[:, 3]], tbl_4[ids[:, 4]], tbl_5[ids[:, 5]], tbl_6[ids[:, 6]], tbl_7[ids[:, 7]], tbl_8[ids[:, 8]], tbl_9[ids[:, 9]], tbl_10[ids[:, 10]], tbl_11[ids[:, 11]], tbl_12[ids[:, 12]], tbl_13[ids[:, 13]], tbl_14[ids[:, 14]], tbl_15[ids[:, 15]], tbl_16[ids[:, 16]], tbl_17[ids[:, 17]], tbl_18[ids[:, 18]], tbl_19[ids[:, 19]], tbl_20[ids[:, 20]], tbl_21[ids[:, 21]], tbl_22[ids[:, 22]], tbl_23[ids[:, 23]], tbl_24[ids[:, 24]], tbl_25[ids[:, 25]], tbl_26[ids[:, 26]], tbl_27[ids[:, 27]], tbl_28[ids[:, 28]], tbl_29[ids[:, 29]], tbl_30[ids[:, 30]], tbl_31[ids[:, 31]]], axis=1)
    z = _L0_rec_ref(e, L0_rec_filter_0, L0_rec_filter_1)
    z = z.reshape(z.shape[0], -1)
    h = jnp.concatenate([z, dense_ctx], axis=1)
    h = jnp.maximum(h @ W_top1 + b_top1, 0.0)
    h = jnp.maximum(h @ W_top2 + b_top2, 0.0)
    y = h @ W_top3
    return y

_drawn_inputs = setup_inputs


def setup_inputs(seed=0):
    import zlib

    import numpy as np

    out = dict(_drawn_inputs(seed))
    spreads = {'b_top1': (0.0, 0.436), 'b_top2': (0.0, 0.431)}
    factors = {'tbl_0': 6.118,
     'tbl_1': 6.193,
     'tbl_2': 6.08,
     'tbl_3': 5.928,
     'tbl_4': 6.005,
     'tbl_5': 6.022,
     'tbl_6': 5.817,
     'tbl_7': 6.122,
     'tbl_8': 5.886,
     'tbl_9': 6.129,
     'tbl_10': 5.696,
     'tbl_11': 6.031,
     'tbl_12': 6.072,
     'tbl_13': 5.72,
     'tbl_14': 6.134,
     'tbl_15': 5.656,
     'tbl_16': 6.329,
     'tbl_17': 5.966,
     'tbl_18': 6.131,
     'tbl_19': 6.443,
     'tbl_20': 6.292,
     'tbl_21': 6.163,
     'tbl_22': 6.124,
     'tbl_23': 6.392,
     'tbl_24': 6.184,
     'tbl_25': 6.12,
     'tbl_26': 6.149,
     'tbl_27': 6.329,
     'tbl_28': 6.286,
     'tbl_29': 6.212,
     'tbl_30': 6.1,
     'tbl_31': 5.788,
     'L0_rec_filter_1': 8.0,
     'dense_ctx': 2.672}
    for name, (base, spread) in spreads.items():
        noise = np.random.default_rng([zlib.crc32(name.encode()), seed]).standard_normal(out[name].shape)
        drawn = base * np.exp(spread * noise) if base else spread * noise
        out[name] = jnp.asarray(drawn.astype(out[name].dtype))
    for name, factor in factors.items():
        out[name] = (out[name] * factor).astype(out[name].dtype)
    return out
```

```python
from contextlib import ExitStack

import concourse.bass as bass
from concourse import mybir

FIELDS, DIM, BATCH = 32, 32, 512
MAPS = 128
QUARTERS = 128 // FIELDS
ROWS = BATCH // QUARTERS
TILES = 4
CHUNKS = ROWS // TILES
COLS = TILES * 128
RUN = TILES * DIM
SHIFTS = 4
GROUPS = 4
BANK = 512
HEADS = BANK // MAPS
BANKS = FIELDS // HEADS
HALF = BANKS // 2
FEEDS = HALF * HEADS
DRING, ARING = 4, 2
CTX, TOP1, TOP2 = 16, 512, 256
T1, T2 = TOP1 // 128, TOP2 // 128
LEAD = 3


def dlrm_tower(nc, table, ids, offsets, dense, w0a, w0b, w0c, w1, wt1, bt1, wt2, bt2, wt3, select, out):
    fp32, f32r, i32 = mybir.dt.float32, mybir.dt.float32r, mybir.dt.int32
    ALU = mybir.AluOpType
    ACT = mybir.ActivationFunctionType
    AX = mybir.AxisListType

    with ExitStack() as ctx:
        def sb(name, shape, dt=fp32):
            return ctx.enter_context(nc.sbuf_tensor(name, shape, dt))

        def sem(name):
            return ctx.enter_context(nc.semaphore(name))

        x_rows = nc.dram_tensor("x_rows", (2, FIELDS + FIELDS // 2, COLS), fp32, kind="Internal").ap()

        raw_ids = sb("raw_ids", [128, ROWS], i32)
        offset = sb("offset", [128, 1], i32)
        all_ids = sb("all_ids", [128, ROWS], i32)
        row_ids = [sb(f"row_ids{p}", [128, TILES], i32) for p in range(2)]
        emb = [sb(f"emb{p}", [128, RUN]) for p in range(2)]
        weigh = [sb(f"weigh{p}", [128, TILES, FIELDS]) for p in range(2)]
        x_same = [sb(f"x_same{p}", [128, COLS]) for p in range(2)]
        x_shift = [sb(f"x_shift{p}", [128, GROUPS, COLS]) for p in range(2)]
        x_last = [sb(f"x_last{p}", [FIELDS, COLS]) for p in range(2)]
        z = [sb(f"z{p}", [128, GROUPS, COLS]) for p in range(2)]
        z_last = [sb(f"z_last{p}", [FIELDS, COLS]) for p in range(2)]
        v = sb("v", [128, GROUPS, MAPS])
        v_b = sb("v_b", [128, GROUPS, MAPS])
        v_last = sb("v_last", [FIELDS, MAPS])
        cur1 = [sb(f"cur1_{p}", [128, COLS]) for p in range(2)]
        cur_hi = [sb(f"cur_hi{p}", [128, COLS], f32r) for p in range(2)]
        cur_lo = [sb(f"cur_lo{p}", [128, COLS], f32r) for p in range(2)]
        w_raw = sb("w_raw", [128, FIELDS * MAPS])
        w_hi = sb("w_hi", [128, FIELDS * MAPS], f32r)
        w_lo = sb("w_lo", [128, FIELDS * MAPS], f32r)
        part = [sb(f"part{p}", [128, TILES, 2, MAPS]) for p in range(2)]
        prod = [sb(f"prod{p}", [128, FEEDS, MAPS]) for p in range(2)]
        side = [sb(f"side{p}", [128, TILES, MAPS]) for p in range(2)]
        both = sb("both", [128, TILES, MAPS])
        whole = sb("whole", [128, TILES, MAPS])
        cur2 = [sb(f"cur2_{p}", [128, TILES, MAPS]) for p in range(2)]
        sel = sb("sel", [128, QUARTERS])
        pool1 = sb("pool1", [128, BATCH])
        pool2 = sb("pool2", [128, BATCH])
        ctx_sb = sb("ctx_sb", [CTX, BATCH])
        wt1_sb = sb("wt1_sb", [128, 2, TOP1])
        wt1_ctx = sb("wt1_ctx", [CTX, TOP1])
        bt1_sb = sb("bt1_sb", [128, T1])
        wt2_sb = sb("wt2_sb", [128, T1, TOP2])
        bt2_sb = sb("bt2_sb", [128, T2])
        wt3_sb = sb("wt3_sb", [128, T2])
        h1 = sb("h1", [128, T1, BATCH])
        h2 = sb("h2", [128, T2, BATCH])
        y_sb = sb("y_sb", [1, BATCH])

        def ps(name):
            return ctx.enter_context(nc.psum_tensor(name, [128, BANK], fp32))

        t_dve = [ps(f"t_dve{r}") for r in range(DRING)]
        t_act = [ps(f"t_act{r}") for r in range(ARING)]
        acc1 = ps("acc1")
        acc_pool2 = ps("acc_pool2")

        ids_loaded, v_loaded, w_loaded, top_loaded = (
            sem("ids_loaded"), sem("v_loaded"), sem("w_loaded"), sem("top_loaded"))
        gathered = [sem(f"gathered{p}") for p in range(2)]
        rows_written = [sem(f"rows_written{p}") for p in range(2)]
        x_loaded = [sem(f"x_loaded{p}") for p in range(2)]
        out_written = sem("out_written")
        ids_ready = sem("ids_ready")
        row_ids_ready = sem("row_ids_ready")
        v_ready, wh_ready, wl_ready = sem("v_ready"), sem("wh_ready"), sem("wl_ready")
        weigh_ready = sem("weigh_ready")
        z_ready = sem("z_ready")
        layer1_done = sem("layer1_done")
        hi_ready, cur1_ready = sem("hi_ready"), sem("cur1_ready")
        lo_ready = sem("lo_ready")
        pool1_ready = sem("pool1_ready")
        dve_bank, act_bank = sem("dve_bank"), sem("act_bank")
        added = sem("added")
        weighed = sem("weighed")
        folded = sem("folded")
        side_ready = sem("side_ready")
        summed = sem("summed")
        cur2_ready = sem("cur2_ready")
        pool2_done = sem("pool2_done")
        pool2_ready = sem("pool2_ready")
        top1_done, top2_done, top3_done = sem("top1_done"), sem("top2_done"), sem("top3_done")
        h1_ready, h2_ready, y_ready = sem("h1_ready"), sem("h2_ready"), sem("y_ready")

        block = ctx.enter_context(nc.Block())

        def wait(eng, s, value):
            if not (isinstance(value, int) and value <= 0):
                eng.wait_ge(s, value)

        def over_chunks(eng, chunk, head=2, tail=2):
            for c in range(head):
                chunk(c, c % 2)
            with eng.Fori(head // 2, (CHUNKS - tail) // 2) as pair:
                for parity in range(2):
                    chunk(pair * 2 + parity, parity)
            for c in range(CHUNKS - tail, CHUNKS):
                chunk(c, c % 2)

        def before(c, parity):
            return (c - parity) // 2

        LOADS = 2 + GROUPS

        @block.sync
        def _(sp):
            sp.dma_start(raw_ids[:, :], ids).then_inc(ids_loaded, 16)
            sp.dma_start(offset[:, :], offsets).then_inc(ids_loaded, 16)

            def chunk(c, p):
                turn = before(c, p) + 1
                wait(sp, layer1_done, c - 1)
                sp.wait_ge(gathered[p], turn * (16 * TILES))
                rows = x_rows[p].rearrange("h (q c) -> q h c", q=QUARTERS)
                for q in range(QUARTERS):
                    sp.dma_start(rows[q, 0:FIELDS], emb[p][q * FIELDS:(q + 1) * FIELDS, :]).then_inc(rows_written[p], 16)
                for q in range(QUARTERS):
                    sp.dma_start(rows[q, FIELDS:FIELDS + FIELDS // 2],
                                 emb[p][q * FIELDS:q * FIELDS + FIELDS // 2, :]).then_inc(rows_written[p], 16)
                sp.wait_ge(rows_written[p], turn * (16 * 2 * QUARTERS))
                src = x_rows[p]
                first, stride = src.offset, COLS
                sp.dma_start(x_same[p][:, :],
                             bass.AP(src.tensor, first, [[0, SHIFTS], [stride, FIELDS], [1, COLS]])).then_inc(x_loaded[p], 16)
                for g in range(GROUPS):
                    sp.dma_start(x_shift[p][:, g, :],
                                 bass.AP(src.tensor, first + g * SHIFTS * stride,
                                         [[stride, SHIFTS], [stride, FIELDS], [1, COLS]])).then_inc(x_loaded[p], 16)
                sp.dma_start(x_last[p][:, :], src[FIELDS // 2:FIELDS + FIELDS // 2, :]).then_inc(x_loaded[p], 16)

            over_chunks(sp, chunk)
            sp.wait_ge(y_ready, 1)
            sp.dma_start(out, y_sb[:, :]).then_inc(out_written, 16)
            sp.wait_ge(out_written, 16)

        @block.gpsimd
        def _(pool):
            def stage(c, p):
                wait(pool, rows_written[p], before(c, p) * (16 * 2 * QUARTERS))
                wait(pool, weigh_ready, c - 1)
                nc.gpsimd.tensor_copy(row_ids[p][:, :], all_ids[:, bass.ds(c * TILES, TILES)]).then_inc(row_ids_ready, 1)

            def gather(p):
                for i in range(TILES):
                    nc.gpsimd.indirect_dma_start(
                        emb[p][:, i * DIM:(i + 1) * DIM], None, table,
                        bass.IndirectOffsetOnAxis(ap=row_ids[p][:, i:i + 1], axis=0)).then_inc(gathered[p], 16)

            def fold(c, i, p, staged=None):
                src = prod[i % 2]
                tile = c * TILES + i
                pool.wait_ge(weighed, (tile + 1) * HALF)
                left, step = FEEDS // 2, 0
                while left > 1:
                    nc.gpsimd.tensor_tensor(src[:, 0:left, :], src[:, 0:left, :], src[:, left:2 * left, :],
                                            ALU.add).then_inc(folded, 1)
                    step += 1
                    pool.wait_ge(folded, tile * 3 + step)
                    left //= 2
                if i == 0:
                    wait(pool, summed, (c - 1) * 2)
                if staged is not None:
                    pool.wait_ge(row_ids_ready, staged + 1)
                nc.gpsimd.tensor_tensor(side[p][:, i, :], src[:, 0, :], src[:, 1, :], ALU.add).then_inc(side_ready, 1)

            pool.wait_ge(ids_ready, 1)
            for c in range(LEAD):
                stage(c, c % 2)
                pool.wait_ge(row_ids_ready, c + 1)
                gather(c % 2)

            def chunk(c, p):
                ahead = not (isinstance(c, int) and c + LEAD >= CHUNKS)
                for i in range(TILES):
                    if ahead and i == 1:
                        stage(c + LEAD, (p + LEAD) % 2)
                    fold(c, i, p, staged=c + LEAD if ahead and i == 1 else None)
                    if ahead and i == 1:
                        gather((p + LEAD) % 2)

            over_chunks(pool, chunk, tail=4)

        @block.scalar
        def _(act):
            act.dma_start(v[:, :, :], w0a).then_inc(v_loaded, 16)
            act.dma_start(v_b[:, :, :], w0b).then_inc(v_loaded, 16)
            act.dma_start(v_last[:, :], w0c).then_inc(v_loaded, 16)
            for k in range(4):
                part_w = slice(k * FIELDS // 4, (k + 1) * FIELDS // 4)
                act.dma_start(w_raw[:, :].rearrange("m (h n) -> m h n", n=MAPS)[:, part_w, :],
                              w1[:, part_w, :]).then_inc(w_loaded, 16)
            act.dma_start(sel[:, :], select).then_inc(top_loaded, 16)
            act.dma_start(ctx_sb[:, :], dense).then_inc(top_loaded, 16)
            act.dma_start(wt1_sb[:, :, :], wt1[0:256, :].rearrange("(k p) n -> p k n", p=128)).then_inc(top_loaded, 16)
            act.dma_start(wt1_ctx[:, :], wt1[256:256 + CTX, :]).then_inc(top_loaded, 16)
            act.dma_start(bt1_sb[:, :], bt1).then_inc(top_loaded, 16)
            act.dma_start(wt2_sb[:, :, :], wt2.rearrange("(k p) n -> p k n", p=128)).then_inc(top_loaded, 16)
            act.dma_start(bt2_sb[:, :], bt2).then_inc(top_loaded, 16)
            act.dma_start(wt3_sb[:, :], wt3).then_inc(top_loaded, 16)
            act.wait_ge(w_loaded, 64)
            nc.scalar.activation(w_hi[:, :], w_raw[:, :], ACT.Copy).then_inc(wh_ready, 1)

            def relu1(c, p):
                act.wait_ge(layer1_done, c + 1)
                wait(act, act_bank, (c - 1) * (TILES * HALF))
                nc.scalar.activation(cur_hi[p][:, :].rearrange("m (i q d) -> m i q d", i=TILES, q=QUARTERS),
                                     acc1[:, :].rearrange("m (q i d) -> m i q d", i=TILES, q=QUARTERS),
                                     ACT.Relu).then_inc(hi_ready, 1)
                wait(act, pool1_ready, c - 1)
                nc.scalar.activation(cur1[p][:, :], acc1[:, :], ACT.Relu).then_inc(cur1_ready, 1)

            def weigh_tile(c, i, p):
                tile = c * TILES + i
                wait(act, side_ready, tile - 1)
                if i == 0:
                    act.wait_ge(weigh_ready, c + 1)
                for k in range(HALF):
                    act.wait_ge(act_bank, tile * HALF + k + 1)
                    for j in range(HEADS):
                        h = HEADS * (2 * k + 1) + j
                        last = nc.scalar.activation(prod[i % 2][:, HEADS * k + j, :],
                                                    t_act[k % ARING][:, j * MAPS:(j + 1) * MAPS], ACT.Copy,
                                                    scale=weigh[p][:, i, h:h + 1])
                    last.then_inc(weighed, 1)

            def chunk(c, p):
                for i in range(TILES):
                    weigh_tile(c, i, p)
                    if i == 1 and not (isinstance(c, int) and c + 1 >= CHUNKS):
                        relu1(c + 1, 1 - p)

            relu1(0, 0)
            over_chunks(act, chunk)

            act.wait_ge(top_loaded, 16 * 8)
            for f in range(T1):
                act.wait_ge(top1_done, f + 1)
                nc.scalar.activation(h1[:, f, :], t_dve[f][:, :], ACT.Relu, bias=bt1_sb[:, f:f + 1]).then_inc(h1_ready, 1)
            for f in range(T2):
                act.wait_ge(top2_done, f + 1)
                nc.scalar.activation(h2[:, f, :], t_act[f][:, :], ACT.Relu, bias=bt2_sb[:, f:f + 1]).then_inc(h2_ready, 1)
            act.wait_ge(top3_done, 1)
            nc.scalar.activation(y_sb[:, :], acc1[0:1, :], ACT.Copy).then_inc(y_ready, 1)

        @block.vector
        def _(dve):
            dve.wait_ge(ids_loaded, 32)
            nc.vector.tensor_tensor(all_ids[:, :], raw_ids[:, :], offset[:, 0:1].to_broadcast([128, ROWS]),
                                    ALU.add).then_inc(ids_ready, 1)

            def transpose(c, p):
                dve.wait_ge(gathered[p], (before(c, p) + 1) * (16 * TILES))
                wait(dve, weighed, (c - 1) * (TILES * HALF))
                wait(dve, added, (c - 1) * (TILES * FEEDS))
                nc.vector.transpose(weigh[p][:, :, :].rearrange("p i h -> p (i h)"), emb[p][:, :]).then_inc(weigh_ready, 1)

            def products(c, p, which):
                if which == 0:
                    dve.wait_ge(x_loaded[p], (before(c, p) + 1) * (16 * LOADS))
                    wait(dve, layer1_done, c - 1)
                if which < 2:
                    g = slice(which * 2, which * 2 + 2)
                    nc.vector.tensor_tensor(z[p][:, g, :], x_shift[p][:, g, :],
                                            x_same[p][:, None, :].to_broadcast([128, 2, COLS]),
                                            ALU.mult).then_inc(z_ready, 1)
                else:
                    nc.vector.tensor_tensor(z_last[p][:, :], x_last[p][:, :], x_same[p][0:FIELDS, :],
                                            ALU.mult).then_inc(z_ready, 1)

            def lower(c, p):
                dve.wait_ge(cur1_ready, c + 1)
                wait(dve, act_bank, (c - 1) * (TILES * HALF))
                nc.vector.tensor_tensor(
                    cur_lo[p][:, :].rearrange("m (i q d) -> m i q d", i=TILES, q=QUARTERS),
                    cur1[p][:, :].rearrange("m (q i d) -> m i q d", i=TILES, q=QUARTERS),
                    cur_hi[p][:, :].bitcast(fp32).rearrange("m (i q d) -> m i q d", i=TILES, q=QUARTERS),
                    ALU.subtract).then_inc(lo_ready, 1)

            def pooling1(c, p):
                dst = pool1[:, bass.ds(c * (TILES * QUARTERS), TILES * QUARTERS)]
                nc.vector.tensor_reduce(dst.rearrange("m (i q) -> m q i", q=QUARTERS),
                                        cur1[p][:, :].rearrange("m (q i d) -> m q i d", i=TILES, q=QUARTERS),
                                        AX.X, ALU.add).then_inc(pool1_ready, 1)

            def add_tile(c, i, p):
                tile = c * TILES + i
                if i == 0:
                    wait(dve, summed, (c - 1) * 2)
                    dve.wait_ge(weigh_ready, c + 1)
                for k in range(HALF):
                    dve.wait_ge(dve_bank, tile * HALF + k + 1)
                    for j in range(HEADS):
                        h, step = HEADS * 2 * k + j, HEADS * k + j
                        src = t_dve[k % DRING][:, j * MAPS:(j + 1) * MAPS]
                        dst = part[p][:, i, step % 2, :]
                        w = weigh[p][:, i, h:h + 1]
                        if step < 2:
                            nc.vector.tensor_scalar(dst, src, w, None, ALU.mult).then_inc(added, 1)
                        else:
                            dve.wait_ge(added, tile * FEEDS + step - 1)
                            nc.vector.scalar_tensor_tensor(dst, src, w, dst, ALU.mult, ALU.add).then_inc(added, 1)

            def finish(c, p):
                dve.wait_ge(added, (c + 1) * (TILES * FEEDS))
                nc.vector.tensor_tensor(both[:, :, :], part[p][:, :, 0, :], part[p][:, :, 1, :], ALU.add).then_inc(summed, 1)
                dve.wait_ge(side_ready, (c + 1) * TILES)
                dve.wait_ge(summed, c * 2 + 1)
                nc.vector.tensor_tensor(whole[:, :, :], both[:, :, :], side[p][:, :, :], ALU.add).then_inc(summed, 1)
                dve.wait_ge(summed, c * 2 + 2)
                wait(dve, pool2_done, c - 1)
                nc.vector.tensor_scalar(cur2[p][:, :, :], whole[:, :, :], 0.0, None, ALU.max).then_inc(cur2_ready, 1)

            def pooling2(c, p):
                dve.wait_ge(pool2_done, c + 1)
                width = TILES * QUARTERS
                nc.vector.tensor_copy(pool2[:, bass.ds(c * width, width)],
                                      acc_pool2[:, 0:width]).then_inc(pool2_ready, 1)

            dve.wait_ge(v_loaded, 48)
            for s in range(1, SHIFTS):
                rows = slice(s * FIELDS, (s + 1) * FIELDS)
                nc.vector.tensor_tensor(v[rows, 0, :], v[rows, 0, :], v_b[rows, 0, :], ALU.add).then_inc(v_ready, 1)
            nc.vector.tensor_tensor(v[:, 1:GROUPS, :], v[:, 1:GROUPS, :], v_b[:, 1:GROUPS, :], ALU.add).then_inc(v_ready, 1)
            transpose(0, 0)
            for which in range(3):
                products(0, 0, which)
            dve.wait_ge(wh_ready, 1)
            nc.vector.tensor_tensor(w_lo[:, :], w_raw[:, :], w_hi[:, :].bitcast(fp32), ALU.subtract).then_inc(wl_ready, 1)
            lower(0, 0)
            pooling1(0, 0)
            for which in range(3):
                products(1, 1, which)

            def chunk(c, p):
                fixed = isinstance(c, int)
                more1, more2 = not (fixed and c + 1 >= CHUNKS), not (fixed and c + 2 >= CHUNKS)
                add_tile(c, 0, p)
                if not (fixed and c == 0):
                    finish(c - 1, 1 - p)
                add_tile(c, 1, p)
                if more1:
                    transpose(c + 1, 1 - p)
                if more2:
                    products(c + 2, p, 0)
                add_tile(c, 2, p)
                if more1:
                    lower(c + 1, 1 - p)
                    pooling1(c + 1, 1 - p)
                if not (fixed and c == 0):
                    pooling2(c - 1, 1 - p)
                add_tile(c, 3, p)
                if more2:
                    products(c + 2, p, 1)
                    products(c + 2, p, 2)

            over_chunks(dve, chunk)
            finish(CHUNKS - 1, (CHUNKS - 1) % 2)
            pooling2(CHUNKS - 1, (CHUNKS - 1) % 2)

        @block.tensor
        def _(pe):
            def layer1(c, p, groups):
                if groups[0] == 0:
                    pe.wait_ge(z_ready, c * 3 + 3)
                    wait(pe, lo_ready, c)
                    wait(pe, cur1_ready, c)
                for g in groups:
                    if g < GROUPS:
                        last = nc.tensor.matmul(acc1[:, :], v[:, g, :], z[p][:, g, :], start=g == 0, stop=False)
                    else:
                        last = nc.tensor.matmul(acc1[:, :], v_last[:, :], z_last[p][:, :], start=False, stop=True)
                if groups[-1] == GROUPS:
                    last.then_inc(layer1_done, 1)

            def layer2(c, i, p):
                tile = c * TILES + i
                cols = slice(i * 128, (i + 1) * 128)
                if i == 0:
                    pe.wait_ge(hi_ready, c + 1)
                    pe.wait_ge(lo_ready, c + 1)
                for k in range(BANKS):
                    n = tile * HALF + k // 2
                    if k % 2 == 0:
                        bank, done = t_dve[(k // 2) % DRING], dve_bank
                        wait(pe, added, (n - DRING + 1) * HEADS)
                    else:
                        bank, done = t_act[(k // 2) % ARING], act_bank
                        wait(pe, weighed, n - ARING + 1)
                    w = slice(k * BANK, (k + 1) * BANK)
                    nc.tensor.matmul(bank[:, :], cur_hi[p][:, cols], w_hi[:, w], start=True, stop=False)
                    nc.tensor.matmul(bank[:, :], cur_hi[p][:, cols], w_lo[:, w], start=False, stop=False)
                    nc.tensor.matmul(bank[:, :], cur_lo[p][:, cols], w_hi[:, w], start=False, stop=True).then_inc(done, 1)

            def pooling(c, p):
                pe.wait_ge(cur2_ready, c + 1)
                wait(pe, pool2_ready, c)
                for i in range(TILES):
                    last = nc.tensor.matmul(acc_pool2[:, i * QUARTERS:(i + 1) * QUARTERS], cur2[p][:, i, :], sel[:, :],
                                            start=True, stop=True)
                last.then_inc(pool2_done, 1)

            pe.wait_ge(v_ready, SHIFTS)
            layer1(0, 0, range(GROUPS + 1))
            pe.wait_ge(wl_ready, 1)
            pe.wait_ge(top_loaded, 16 * 8)

            def chunk(c, p):
                fixed = isinstance(c, int)
                more = not (fixed and c + 1 >= CHUNKS)
                layer2(c, 0, p)
                if more:
                    layer1(c + 1, 1 - p, range(0, 2))
                layer2(c, 1, p)
                if more:
                    layer1(c + 1, 1 - p, range(2, GROUPS + 1))
                layer2(c, 2, p)
                if not (fixed and c == 0):
                    pooling(c - 1, 1 - p)
                layer2(c, 3, p)

            over_chunks(pe, chunk)
            pooling(CHUNKS - 1, (CHUNKS - 1) % 2)

            pe.wait_ge(added, CHUNKS * TILES * FEEDS)
            pe.wait_ge(weighed, CHUNKS * TILES * HALF)
            pe.wait_ge(pool1_ready, CHUNKS)
            pe.wait_ge(pool2_ready, CHUNKS)
            for f in range(T1):
                cols = slice(f * 128, (f + 1) * 128)
                nc.tensor.matmul(t_dve[f][:, :], wt1_ctx[:, cols], ctx_sb[:, :], start=True, stop=False)
                nc.tensor.matmul(t_dve[f][:, :], wt1_sb[:, 0, cols], pool1[:, :], start=False, stop=False)
                nc.tensor.matmul(t_dve[f][:, :], wt1_sb[:, 1, cols], pool2[:, :], start=False,
                                 stop=True).then_inc(top1_done, 1)
            for f in range(T2):
                for k in range(T1):
                    if f == 0:
                        pe.wait_ge(h1_ready, k + 1)
                    last = nc.tensor.matmul(t_act[f][:, :], wt2_sb[:, k, f * 128:(f + 1) * 128], h1[:, k, :],
                                            start=k == 0, stop=k == T1 - 1)
                last.then_inc(top2_done, 1)
            for k in range(T2):
                pe.wait_ge(h2_ready, k + 1)
                last = nc.tensor.matmul(acc1[0:1, :], wt3_sb[:, k:k + 1], h2[:, k, :], start=k == 0, stop=k == T2 - 1)
            last.then_inc(top3_done, 1)


def kernel(**inputs):
    import numpy as np
    import concourse.bacc as bacc
    from concourse import mybir
    from concourse.bass_utils import run_bass_kernel_spmd

    def host(name):
        return np.asarray(inputs[name])

    tables = [host(f"tbl_{f}") for f in range(FIELDS)]
    starts = np.concatenate([[0], np.cumsum([t.shape[0] for t in tables])[:-1]]).astype(np.int32)
    shift, field = np.arange(SHIFTS * GROUPS)[:, None], np.arange(FIELDS)[None, :]
    w0 = host("L0_rec_filter_0").reshape(FIELDS, FIELDS, MAPS)

    def by_group(a):
        return a.reshape(GROUPS, SHIFTS * FIELDS, MAPS).transpose(1, 0, 2)

    arrays = {
        "table": np.concatenate(tables),
        "ids": host("ids").reshape(QUARTERS, ROWS, FIELDS).transpose(0, 2, 1).reshape(128, ROWS),
        "offsets": np.tile(starts, QUARTERS)[:, None],
        "dense": host("dense_ctx").reshape(QUARTERS, ROWS, CTX).transpose(2, 1, 0).reshape(CTX, BATCH),
        "w0a": by_group(w0[field, (field + shift) % FIELDS]),
        "w0b": by_group(w0[(field + shift) % FIELDS, field]),
        "w0c": w0[np.arange(FIELDS), (np.arange(FIELDS) + FIELDS // 2) % FIELDS],
        "w1": host("L0_rec_filter_1").reshape(FIELDS, MAPS, MAPS).transpose(1, 0, 2),
        "wt1": host("W_top1"),
        "bt1": host("b_top1").reshape(T1, 128).T,
        "wt2": host("W_top2"),
        "bt2": host("b_top2").reshape(T2, 128).T,
        "wt3": host("W_top3").reshape(T2, 128).T,
        "select": np.repeat(np.eye(QUARTERS, dtype=np.float32), DIM, axis=0),
    }
    nc = bacc.Bacc("TRN2", target_bir_lowering=False, num_devices=1)
    given, args = {}, []
    for name, a in arrays.items():
        a = np.ascontiguousarray(a)
        given[f"{name}_dram"] = a
        args.append(nc.dram_tensor(f"{name}_dram", a.shape, mybir.dt.from_np(a.dtype), kind="ExternalInput").ap())
    args.append(nc.dram_tensor("y_dram", (1, BATCH), mybir.dt.float32, kind="ExternalOutput").ap())
    dlrm_tower(nc, *args)
    result = run_bass_kernel_spmd(nc, [given], core_ids=[0])
    y = result.results[0]["y_dram"]
    return y.reshape(ROWS, QUARTERS).T.reshape(BATCH, 1)
```

```python
from contextlib import ExitStack

import concourse.bass as bass
from concourse import mybir

FIELDS, DIM, BATCH = 32, 32, 512
MAPS = 128
QUARTERS = 128 // FIELDS
ROWS = BATCH // QUARTERS
TILES = 4
CHUNKS = ROWS // TILES
COLS = TILES * 128
RUN = TILES * DIM
SHIFTS = 4
GROUPS = 4
SPLIT = 2
WHOLE = GROUPS - SPLIT
BANK = 512
V_SUMS = [(slice(0, FIELDS), slice(1, GROUPS)), (slice(FIELDS, 2 * FIELDS), slice(0, GROUPS)),
          (slice(2 * FIELDS, 4 * FIELDS), slice(0, GROUPS))]
HEADS = BANK // MAPS
BANKS = FIELDS // HEADS
HALF = BANKS // 2
FEEDS = HALF * HEADS
DRING, ARING = 4, 2
SEL_WIDE = 2 * 128 - QUARTERS
CTX, TOP1, TOP2 = 16, 512, 256
T1, T2 = TOP1 // 128, TOP2 // 128
W_PIECES = BANKS
W_EARLY = 5
W_PIECE = FIELDS * MAPS // W_PIECES
FOLDS = [(slice(2, 9), slice(9, 16)), (slice(2, 5), slice(5, 8)), (slice(2, 4), slice(4, 9, 4))]
WARM_UPS = 14
LEAD = 3


def dlrm_tower(nc, table, ids, dense, w0a, w0b, w0c, w1, wt1, bt1, wt2, bt2, wt3, select, identity, out):
    fp32, f32r, i32 = mybir.dt.float32, mybir.dt.float32r, mybir.dt.int32
    ALU = mybir.AluOpType
    ACT = mybir.ActivationFunctionType
    AX = mybir.AxisListType

    with ExitStack() as ctx:
        def sb(name, shape, dt=fp32):
            return ctx.enter_context(nc.sbuf_tensor(name, shape, dt))

        def sem(name):
            return ctx.enter_context(nc.semaphore(name))

        x_rows = nc.dram_tensor("x_rows", (2, 2 * FIELDS, COLS), fp32, kind="Internal").ap()

        raw_ids = sb("raw_ids", [128, ROWS + 1], i32)
        all_ids = sb("all_ids", [128, ROWS], i32)
        row_ids = [sb(f"row_ids{p}", [128, TILES], i32) for p in range(2)]
        emb = [sb(f"emb{p}", [128, RUN]) for p in range(2)]
        weigh = [sb(f"weigh{p}", [128, TILES, FIELDS]) for p in range(2)]
        x_same = [sb(f"x_same{p}", [128, COLS]) for p in range(2)]
        x_shift = [sb(f"x_shift{p}", [128, GROUPS, COLS]) for p in range(2)]
        x_last = [sb(f"x_last{p}", [3 * FIELDS, COLS]) for p in range(2)]
        z = [sb(f"z{p}", [128, GROUPS, COLS]) for p in range(2)]
        z_last = [sb(f"z_last{p}", [3 * FIELDS, COLS]) for p in range(2)]
        z_hi = sb("z_hi", [128, SPLIT, COLS], f32r)
        z_lo = sb("z_lo", [128, SPLIT, COLS], f32r)
        z_parts = [sb(f"z_parts{p}", [3 * FIELDS, COLS], f32r) for p in range(2)]
        v = sb("v", [128, GROUPS, MAPS])
        v_b = sb("v_b", [128, GROUPS, MAPS])
        v_last = sb("v_last", [3 * FIELDS, MAPS])
        v_hi = sb("v_hi", [128, SPLIT, MAPS], f32r)
        v_lo = sb("v_lo", [128, SPLIT, MAPS], f32r)
        v_parts = sb("v_parts", [3 * FIELDS, MAPS], f32r)
        cur1 = [sb(f"cur1_{p}", [128, COLS]) for p in range(2)]
        cur_hi = [sb(f"cur_hi{p}", [128, COLS], f32r) for p in range(2)]
        cur_lo = [sb(f"cur_lo{p}", [128, COLS], f32r) for p in range(2)]
        w_raw = sb("w_raw", [128, FIELDS * MAPS])
        w_hi = sb("w_hi", [128, FIELDS * MAPS], f32r)
        w_lo = sb("w_lo", [128, FIELDS * MAPS], f32r)
        part = [sb(f"part{p}", [128, TILES, 2, MAPS]) for p in range(2)]
        prod = [sb(f"prod{i}", [128, FEEDS, MAPS]) for i in range(TILES)]
        side = [sb(f"side{p}", [128, TILES, MAPS]) for p in range(2)]
        both = sb("both", [128, TILES, MAPS])
        whole = sb("whole", [128, TILES, MAPS])
        cur2_hi = [sb(f"cur2_hi{p}", [128, TILES, MAPS], f32r) for p in range(2)]
        cur2_lo = [sb(f"cur2_lo{p}", [128, TILES, MAPS], f32r) for p in range(2)]
        sel_wide = sb("sel_wide", [128, SEL_WIDE])
        sel = [sb(f"sel{p}", [128, 128], f32r) for p in range(2)]
        ident = sb("ident", [128, 128])
        pool1 = sb("pool1", [128, TILES, CHUNKS * QUARTERS])
        pool2_rows = sb("pool2_rows", [128, TILES, MAPS])
        pool2 = sb("pool2", [128, BATCH])
        ctx_sb = sb("ctx_sb", [CTX, BATCH])
        wt1_sb = sb("wt1_sb", [128, 2, TOP1])
        wt1_ctx = sb("wt1_ctx", [CTX, TOP1])
        bt1_sb = sb("bt1_sb", [128, T1])
        wt2_sb = sb("wt2_sb", [128, T1, TOP2])
        bt2_sb = sb("bt2_sb", [128, T2])
        wt3_sb = sb("wt3_sb", [128, T2])
        h1 = w_raw[:, 0:T1 * BATCH].rearrange("n (f b) -> n f b", f=T1)
        h2 = w_raw[:, T1 * BATCH:(T1 + T2) * BATCH].rearrange("n (f b) -> n f b", f=T2)
        y_sb = sb("y_sb", [1, BATCH])

        def ps(name):
            return ctx.enter_context(nc.psum_tensor(name, [128, BANK], fp32))

        t_dve = [ps(f"t_dve{r}") for r in range(DRING)]
        t_act = [ps(f"t_act{r}") for r in range(ARING)]
        acc1 = ps("acc1")
        acc_pool2 = ps("acc_pool2")

        ids_loaded, v_loaded, sel_loaded, top_loaded = (
            sem("ids_loaded"), sem("v_loaded"), sem("sel_loaded"), sem("top_loaded"))
        w_loaded = [sem(f"w_loaded{k}") for k in range(W_PIECES)]
        gathered = [sem(f"gathered{p}") for p in range(2)]
        rows_written = [sem(f"rows_written{p}") for p in range(2)]
        x_first = [sem(f"x_first{p}") for p in range(2)]
        x_rest = [sem(f"x_rest{p}") for p in range(2)]
        out_written = sem("out_written")
        ids_ready = sem("ids_ready")
        row_ids_ready = sem("row_ids_ready")
        v_ready, wh_ready, wl_ready = sem("v_ready"), sem("wh_ready"), sem("wl_ready")
        weigh_ready = sem("weigh_ready")
        z_ready = sem("z_ready")
        z_rounded = sem("z_rounded")
        pair_rounded = sem("pair_rounded")
        z_parts_ready = sem("z_parts_ready")
        z_lo_ready = sem("z_lo_ready")
        layer1_done = sem("layer1_done")
        hi_ready, cur1_ready = sem("hi_ready"), sem("cur1_ready")
        lo_ready = sem("lo_ready")
        pool1_ready = sem("pool1_ready")
        dve_bank, act_bank = sem("dve_bank"), sem("act_bank")
        added = sem("added")
        weighed = sem("weighed")
        folded = sem("folded")
        side_ready = sem("side_ready")
        summed = sem("summed")
        sel_ready = sem("sel_ready")
        cur2_hi_ready = sem("cur2_hi_ready")
        cur2_ready = sem("cur2_ready")
        pool2_done = sem("pool2_done")
        pool2_rows_ready, pool2_turned, pool2_ready = sem("pool2_rows_ready"), sem("pool2_turned"), sem("pool2_ready")
        top1_done, top2_done, top3_done = sem("top1_done"), sem("top2_done"), sem("top3_done")
        h1_ready, h2_ready, y_ready = sem("h1_ready"), sem("h2_ready"), sem("y_ready")

        block = ctx.enter_context(nc.Block())

        def wait(eng, s, value):
            if not (isinstance(value, int) and value <= 0):
                eng.wait_ge(s, value)

        def over_chunks(eng, chunk, head=2, tail=2, after_head=None):
            for c in range(head):
                chunk(c, c % 2)
            if after_head is not None:
                after_head()
            with eng.Fori(head // 2, (CHUNKS - tail) // 2) as pair:
                for parity in range(2):
                    chunk(pair * 2 + parity, parity)
            for c in range(CHUNKS - tail, CHUNKS):
                chunk(c, c % 2)

        def before(c, parity):
            return (c - parity) // 2

        @block.sync
        def _(sp):
            sp.dma_start(raw_ids[:, :], ids).then_inc(ids_loaded, 16)

            def chunk(c, p):
                turn = before(c, p) + 1
                wait(sp, layer1_done, c - 1)
                sp.wait_ge(gathered[p], turn * (16 * TILES))
                rows = x_rows[p].rearrange("h (q c) -> q h c", q=QUARTERS)
                sp.dma_start(rows[:, 0:FIELDS], emb[p][:, :]).then_inc(rows_written[p], 16)
                sp.dma_start(rows[:, FIELDS:2 * FIELDS], emb[p][:, :]).then_inc(rows_written[p], 16)
                sp.wait_ge(rows_written[p], turn * (16 * 2))
                src = x_rows[p]
                first, stride = src.offset, COLS
                sp.dma_start(x_same[p][:, :],
                             bass.AP(src.tensor, first, [[0, SHIFTS], [stride, FIELDS], [1, COLS]])).then_inc(x_first[p], 16)
                def shifted(first_group, groups):
                    return bass.AP(src.tensor, first + first_group * stride,
                                   [[GROUPS * stride, SHIFTS], [stride, FIELDS], [1, groups * COLS]])

                sp.dma_start(x_shift[p][:, 0:WHOLE, :].rearrange("p g c -> p (g c)"),
                             shifted(0, WHOLE)).then_inc(x_first[p], 16)
                sp.dma_start(x_last[p][:, :],
                             bass.AP(src.tensor, first + FIELDS // 2 * stride,
                                     [[0, 3], [stride, FIELDS], [1, COLS]])).then_inc(x_rest[p], 16)
                sp.dma_start(x_shift[p][:, WHOLE:GROUPS, :].rearrange("p g c -> p (g c)"),
                             shifted(WHOLE, SPLIT)).then_inc(x_rest[p], 16)

            def top_loads():
                sp.dma_start(ctx_sb[:, :], dense).then_inc(top_loaded, 16)
                sp.dma_start(ident[:, :], identity).then_inc(top_loaded, 16)
                sp.dma_start(wt1_sb[:, :, :], wt1[0:256, :].rearrange("(k p) n -> p k n", p=128)).then_inc(top_loaded, 16)
                sp.dma_start(wt1_ctx[:, :], wt1[256:256 + CTX, :]).then_inc(top_loaded, 16)
                sp.dma_start(bt1_sb[:, :], bt1).then_inc(top_loaded, 16)
                sp.dma_start(wt2_sb[:, :, :], wt2.rearrange("(k p) n -> p k n", p=128)).then_inc(top_loaded, 16)
                sp.dma_start(bt2_sb[:, :], bt2).then_inc(top_loaded, 16)
                sp.dma_start(wt3_sb[:, :], wt3).then_inc(top_loaded, 16)

            over_chunks(sp, chunk, after_head=top_loads)
            sp.wait_ge(y_ready, 1)
            sp.dma_start(out, y_sb[:, :]).then_inc(out_written, 16)
            sp.wait_ge(out_written, 16)

        @block.gpsimd
        def _(pool):
            def stage(c, p):
                wait(pool, rows_written[p], before(c, p) * (16 * 2))
                wait(pool, weigh_ready, c - 1)
                nc.gpsimd.tensor_copy(row_ids[p][:, :], all_ids[:, bass.ds(c * TILES, TILES)]).then_inc(row_ids_ready, 1)

            def gather(p, which):
                for i in which:
                    nc.gpsimd.indirect_dma_start(
                        emb[p][:, i * DIM:(i + 1) * DIM], None, table,
                        bass.IndirectOffsetOnAxis(ap=row_ids[p][:, i:i + 1], axis=0)).then_inc(gathered[p], 16)

            def lower_last(c, p):
                low = slice(0, FIELDS)
                pool.wait_ge(z_rounded, c + 1)
                nc.gpsimd.tensor_tensor(z_parts[p][low, :], z_last[p][low, :], z_parts[p][low, :].bitcast(fp32),
                                        ALU.subtract).then_inc(z_parts_ready, 1)

            def lower_pair(c, p):
                pool.wait_ge(pair_rounded, c)
                pool.wait_ge(layer1_done, c)
                nc.gpsimd.tensor_tensor(z_lo[:, 0, :], z[p][:, WHOLE, :], z_hi[:, 0, :].bitcast(fp32),
                                        ALU.subtract).then_inc(z_parts_ready, 1)

            def fold(c, i, p, staged=None):
                src = prod[i]
                tile = c * TILES + i
                pool.wait_ge(weighed, (tile + 1) * HALF)
                for step, (dst, other) in enumerate(FOLDS):
                    if step > 0:
                        pool.wait_ge(folded, tile * len(FOLDS) + step)
                    nc.gpsimd.tensor_tensor(src[:, dst, :], src[:, dst, :], src[:, other, :], ALU.add).then_inc(folded, 1)
                pool.wait_ge(folded, (tile + 1) * len(FOLDS))
                if i == 0:
                    wait(pool, summed, (c - 1) * 2)
                if staged is not None:
                    pool.wait_ge(row_ids_ready, staged + 1)
                nc.gpsimd.tensor_tensor(side[p][:, i, :], src[:, 2, :], src[:, 3, :], ALU.add).then_inc(side_ready, 1)

            pool.wait_ge(ids_ready, 1)
            for c in range(LEAD):
                stage(c, c % 2)
                pool.wait_ge(row_ids_ready, c + 1)
                gather(c % 2, range(TILES))
            lower_last(0, 0)
            lower_last(1, 1)

            def chunk(c, p):
                ahead = not (isinstance(c, int) and c + LEAD >= CHUNKS)
                if not (isinstance(c, int) and c + 1 >= CHUNKS):
                    lower_pair(c + 1, 1 - p)
                for i in range(TILES):
                    if ahead and i == 0:
                        stage(c + LEAD, (p + LEAD) % 2)
                    fold(c, i, p, staged=c + LEAD if ahead and i == 0 else None)
                    if ahead:
                        gather((p + LEAD) % 2, ((0,), (1,), (2, 3), ())[i])
                if not (isinstance(c, int) and c + 2 >= CHUNKS):
                    lower_last(c + 2, p)

            over_chunks(pool, chunk, tail=4)

        @block.scalar
        def _(act):
            act.dma_start(v[:, :, :], w0a).then_inc(v_loaded, 16)
            act.dma_start(v_b[:, :, :], w0b).then_inc(v_loaded, 16)
            act.dma_start(v_last[:, :], bass.AP(w0c.tensor, w0c.offset, [[0, 3], [MAPS, FIELDS], [1, MAPS]])
                          ).then_inc(v_loaded, 16)
            act.dma_start(sel_wide[:, :], select).then_inc(sel_loaded, 16)
            def load_w(k):
                w = slice(k * W_PIECE, (k + 1) * W_PIECE)
                act.dma_start(w_raw[:, w], w1[:, w]).then_inc(w_loaded[k], 16)

            def upper_w(k):
                w = slice(k * W_PIECE, (k + 1) * W_PIECE)
                act.wait_ge(w_loaded[k], 16)
                nc.scalar.activation(w_hi[:, w], w_raw[:, w], ACT.Copy).then_inc(wh_ready, 1)

            def relu1(c, p):
                act.wait_ge(layer1_done, c + 1)
                wait(act, act_bank, (c - 1) * (TILES * HALF))
                nc.scalar.activation(cur_hi[p][:, :].rearrange("m (i q d) -> m i q d", i=TILES, q=QUARTERS),
                                     acc1[:, :].rearrange("m (q i d) -> m i q d", i=TILES, q=QUARTERS),
                                     ACT.Relu).then_inc(hi_ready, 1)
                wait(act, pool1_ready, c - 1)
                nc.scalar.activation(cur1[p][:, :], acc1[:, :], ACT.Relu).then_inc(cur1_ready, 1)

            def round_last(c, p):
                act.wait_ge(z_ready, c * 3 + 2)
                wait(act, layer1_done, c - 1)
                nc.scalar.activation(z_parts[p][:, :], z_last[p][:, :], ACT.Copy).then_inc(z_rounded, 1)

            def round_pair(c, p):
                act.wait_ge(z_ready, c * 3 + 3)
                act.wait_ge(layer1_done, c)
                nc.scalar.activation(z_hi[:, :, :], z[p][:, WHOLE:GROUPS, :], ACT.Copy).then_inc(pair_rounded, 1)

            def relu2(c, p):
                act.wait_ge(summed, c * 2 + 2)
                wait(act, pool2_done, c - 1)
                nc.scalar.activation(cur2_hi[p][:, :, :], whole[:, :, :], ACT.Relu).then_inc(cur2_hi_ready, 1)

            def weigh_tile(c, i, p):
                tile = c * TILES + i
                wait(act, side_ready, tile - TILES + 1)
                wait(act, added, (tile - TILES) * FEEDS + 2)
                if i == 0:
                    act.wait_ge(weigh_ready, c + 1)
                for k in range(HALF):
                    act.wait_ge(act_bank, tile * HALF + k + 1)
                    for j in range(HEADS):
                        h = HEADS * 2 * k + j
                        last = nc.scalar.activation(prod[i][:, HEADS * k + j, :],
                                                    t_act[k % ARING][:, j * MAPS:(j + 1) * MAPS], ACT.Copy,
                                                    scale=weigh[p][:, i, h:h + 1])
                    last.then_inc(weighed, 1)

            def chunk(c, p):
                for i in range(TILES):
                    weigh_tile(c, i, p)
                    if i == 0 and isinstance(c, int) and c == 0:
                        round_last(1, 1)
                    if i == 0 and not (isinstance(c, int) and c + 1 >= CHUNKS):
                        round_pair(c + 1, 1 - p)
                    if i == 1 and not (isinstance(c, int) and c == 0):
                        relu2(c - 1, 1 - p)
                    if i == 1 and not (isinstance(c, int) and c + 1 >= CHUNKS):
                        relu1(c + 1, 1 - p)
                    if i == 2 and not (isinstance(c, int) and c + 2 >= CHUNKS):
                        round_last(c + 2, p)

            for k in range(W_EARLY):
                load_w(k)
            for k in range(W_EARLY):
                upper_w(k)
            act.wait_ge(x_rest[0], 16 * 2)
            for k in range(W_EARLY, W_PIECES):
                load_w(k)
            round_last(0, 0)
            upper_w(W_EARLY)
            relu1(0, 0)
            for k in range(W_EARLY + 1, W_PIECES):
                upper_w(k)
            over_chunks(act, chunk)
            relu2(CHUNKS - 1, (CHUNKS - 1) % 2)

            act.wait_ge(top_loaded, 16 * 8)
            for f in range(T1):
                act.wait_ge(top1_done, f + 1)
                nc.scalar.activation(h1[:, f, :], t_dve[f][:, :], ACT.Relu, bias=bt1_sb[:, f:f + 1]).then_inc(h1_ready, 1)
            for f in range(T2):
                act.wait_ge(top2_done, f + 1)
                nc.scalar.activation(h2[:, f, :], t_act[f][:, :], ACT.Relu, bias=bt2_sb[:, f:f + 1]).then_inc(h2_ready, 1)
            act.wait_ge(top3_done, 1)
            nc.scalar.activation(y_sb[:, :], acc1[0:1, :], ACT.Copy).then_inc(y_ready, 1)

        @block.vector
        def _(dve):
            dve.wait_ge(ids_loaded, 16)
            nc.vector.tensor_tensor(all_ids[:, :], raw_ids[:, 0:ROWS], raw_ids[:, ROWS:ROWS + 1].to_broadcast([128, ROWS]),
                                    ALU.add).then_inc(ids_ready, 1)

            def transpose(c, p):
                dve.wait_ge(gathered[p], (before(c, p) + 1) * (16 * TILES))
                wait(dve, weighed, (c - 1) * (TILES * HALF))
                wait(dve, added, (c - 1) * (TILES * FEEDS))
                nc.vector.transpose(weigh[p][:, :, :].rearrange("p i h -> p (i h)"), emb[p][:, :]).then_inc(weigh_ready, 1)

            def products(c, p, which):
                turn = before(c, p) + 1
                if which == 0:
                    dve.wait_ge(x_first[p], turn * (16 * 2))
                    wait(dve, layer1_done, c - 1)
                elif which == 2:
                    dve.wait_ge(x_rest[p], turn * (16 * 2))
                if which < 2:
                    g = slice(which * 2, which * 2 + 2)
                    nc.vector.tensor_tensor(z[p][:, g, :], x_shift[p][:, g, :],
                                            x_same[p][:, None, :].to_broadcast([128, 2, COLS]),
                                            ALU.mult).then_inc(z_ready, 1)
                else:
                    nc.vector.tensor_tensor(z_last[p][:, :], x_last[p][:, :], x_same[p][0:3 * FIELDS, :],
                                            ALU.mult).then_inc(z_ready, 1)

            def lower_pair(c, p):
                dve.wait_ge(pair_rounded, c)
                dve.wait_ge(layer1_done, c)
                nc.vector.tensor_tensor(z_lo[:, 1, :], z[p][:, WHOLE + 1, :], z_hi[:, 1, :].bitcast(fp32),
                                        ALU.subtract).then_inc(z_lo_ready, 1)

            def lower(c, p):
                dve.wait_ge(cur1_ready, c + 1)
                wait(dve, act_bank, (c - 1) * (TILES * HALF))
                nc.vector.tensor_tensor(
                    cur_lo[p][:, :].rearrange("m (i q d) -> m i q d", i=TILES, q=QUARTERS),
                    cur1[p][:, :].rearrange("m (q i d) -> m i q d", i=TILES, q=QUARTERS),
                    cur_hi[p][:, :].bitcast(fp32).rearrange("m (i q d) -> m i q d", i=TILES, q=QUARTERS),
                    ALU.subtract).then_inc(lo_ready, 1)

            def pooling1(c, p):
                dst = pool1[:, :, bass.ds(c * QUARTERS, QUARTERS)]
                nc.vector.tensor_reduce(dst.rearrange("m i q -> m q i"),
                                        cur1[p][:, :].rearrange("m (q i d) -> m q i d", i=TILES, q=QUARTERS),
                                        AX.X, ALU.add).then_inc(pool1_ready, 1)

            def add_tile(c, i, p):
                tile = c * TILES + i
                if i == 0:
                    wait(dve, summed, (c - 1) * 2)
                    dve.wait_ge(weigh_ready, c + 1)
                for k in range(HALF):
                    dve.wait_ge(dve_bank, tile * HALF + k + 1)
                    for j in range(HEADS):
                        h, step = HEADS * (2 * k + 1) + j, HEADS * k + j
                        src = t_dve[k % DRING][:, j * MAPS:(j + 1) * MAPS]
                        dst = part[p][:, i, step % 2, :]
                        w = weigh[p][:, i, h:h + 1]
                        if step < 2:
                            if step == 0:
                                dve.wait_ge(weighed, tile * HALF + 1)
                            nc.vector.scalar_tensor_tensor(dst, src, w, prod[i][:, step, :],
                                                           ALU.mult, ALU.add).then_inc(added, 1)
                        else:
                            dve.wait_ge(added, tile * FEEDS + step - 1)
                            nc.vector.scalar_tensor_tensor(dst, src, w, dst, ALU.mult, ALU.add).then_inc(added, 1)

            def finish(c, p):
                dve.wait_ge(added, (c + 1) * (TILES * FEEDS))
                nc.vector.tensor_tensor(both[:, :, :], part[p][:, :, 0, :], part[p][:, :, 1, :], ALU.add).then_inc(summed, 1)
                dve.wait_ge(side_ready, (c + 1) * TILES)
                dve.wait_ge(summed, c * 2 + 1)
                wait(dve, cur2_hi_ready, c)
                nc.vector.tensor_tensor(whole[:, :, :], both[:, :, :], side[p][:, :, :], ALU.add).then_inc(summed, 1)

            def lower2(c, p):
                dve.wait_ge(summed, c * 2 + 2)
                dve.wait_ge(cur2_hi_ready, c + 1)
                wait(dve, pool2_done, c - 1)
                nc.vector.scalar_tensor_tensor(cur2_lo[p][:, :, :], whole[:, :, :], 0.0,
                                               cur2_hi[p][:, :, :].bitcast(fp32), ALU.max,
                                               ALU.subtract).then_inc(cur2_ready, 1)

            def place(c, p):
                wait(dve, pool2_done, c - 1)
                nc.vector.tensor_copy(sel[p][:, :], sel_wide[:, bass.ds(c * -QUARTERS + (CHUNKS - 1) * QUARTERS, 128)]
                                      ).then_inc(sel_ready, 1)

            dve.wait_ge(v_loaded, 48)
            for rows, groups in V_SUMS:
                nc.vector.tensor_tensor(v[rows, groups, :], v[rows, groups, :], v_b[rows, groups, :],
                                        ALU.add).then_inc(v_ready, 1)
            nc.vector.tensor_copy(v_parts[:, :], v_last[:, :]).then_inc(v_ready, 1)
            low = slice(2 * FIELDS, 3 * FIELDS)
            dve.wait_ge(v_ready, len(V_SUMS) + 1)
            nc.vector.tensor_tensor(v_parts[low, :], v_last[low, :], v_parts[low, :].bitcast(fp32),
                                    ALU.subtract).then_inc(v_ready, 1)
            nc.vector.tensor_copy(v_hi[:, :, :], v[:, WHOLE:GROUPS, :]).then_inc(v_ready, 1)
            dve.wait_ge(v_ready, len(V_SUMS) + 3)
            nc.vector.tensor_tensor(v_lo[:, :, :], v[:, WHOLE:GROUPS, :], v_hi[:, :, :].bitcast(fp32),
                                    ALU.subtract).then_inc(v_ready, 1)
            dve.wait_ge(sel_loaded, 16)
            transpose(0, 0)
            def lower_w(k):
                w = slice(k * W_PIECE, (k + 1) * W_PIECE)
                dve.wait_ge(wh_ready, k + 1)
                nc.vector.tensor_tensor(w_lo[:, w], w_raw[:, w], w_hi[:, w].bitcast(fp32), ALU.subtract).then_inc(wl_ready, 1)

            for k in range(W_EARLY):
                lower_w(k)
            for which in (0, 2, 1):
                products(0, 0, which)
            lower_w(W_EARLY)
            lower(0, 0)
            for k in range(W_EARLY + 1, W_PIECES):
                lower_w(k)
            pooling1(0, 0)
            for which in (0, 2, 1):
                products(1, 1, which)

            def chunk(c, p):
                fixed = isinstance(c, int)
                more1, more2 = not (fixed and c + 1 >= CHUNKS), not (fixed and c + 2 >= CHUNKS)
                if more1:
                    transpose(c + 1, 1 - p)
                add_tile(c, 0, p)
                if more1:
                    lower_pair(c + 1, 1 - p)
                if not (fixed and c == 0):
                    finish(c - 1, 1 - p)
                add_tile(c, 1, p)
                if not (fixed and c == 0):
                    lower2(c - 1, 1 - p)
                if more2:
                    products(c + 2, p, 0)
                    products(c + 2, p, 2)
                add_tile(c, 2, p)
                if more1:
                    lower(c + 1, 1 - p)
                    pooling1(c + 1, 1 - p)
                place(c, p)
                add_tile(c, 3, p)
                if more2:
                    products(c + 2, p, 1)

            over_chunks(dve, chunk)
            finish(CHUNKS - 1, (CHUNKS - 1) % 2)
            lower2(CHUNKS - 1, (CHUNKS - 1) % 2)
            dve.wait_ge(pool2_done, CHUNKS)
            nc.vector.tensor_copy(pool2_rows[:, :, :].rearrange("p i n -> p (i n)"), acc_pool2[:, :]).then_inc(pool2_rows_ready, 1)
            dve.wait_ge(pool2_turned, 1)
            nc.vector.tensor_copy(pool2[:, :], t_act[0][:, :]).then_inc(pool2_ready, 1)

        @block.tensor
        def _(pe):
            def layer1(c, p, groups):
                if groups[0] == 0:
                    wait(pe, lo_ready, c)
                    wait(pe, cur1_ready, c)
                for g in groups:
                    if g < WHOLE or (g < GROUPS and isinstance(c, int) and c == 0):
                        if g == 0:
                            pe.wait_ge(z_ready, c * 3 + 1)
                        elif g == WHOLE:
                            pe.wait_ge(z_ready, 3)
                        nc.tensor.matmul(acc1[:, :], v[:, g, :], z[p][:, g, :], start=g == 0, stop=False)
                    elif g < GROUPS:
                        k = g - WHOLE
                        if k == 0:
                            pe.wait_ge(z_parts_ready, c * 2 + 1)
                        else:
                            pe.wait_ge(z_lo_ready, c)
                        nc.tensor.matmul(acc1[:, :], v_hi[:, k, :], z_hi[:, k, :], start=False, stop=False)
                        nc.tensor.matmul(acc1[:, :], v_lo[:, k, :], z_hi[:, k, :], start=False, stop=False)
                        nc.tensor.matmul(acc1[:, :], v_hi[:, k, :], z_lo[:, k, :], start=False, stop=False)
                    else:
                        pe.wait_ge(z_parts_ready, c * 2 + 1)
                        nc.tensor.matmul(acc1[:, :], v_parts[:, :], z_parts[p][:, :], start=False,
                                         stop=True).then_inc(layer1_done, 1)

            def layer2(c, i, p):
                tile = c * TILES + i
                cols = slice(i * 128, (i + 1) * 128)
                if i == 0:
                    pe.wait_ge(hi_ready, c + 1)
                    pe.wait_ge(lo_ready, c + 1)
                for k in range(BANKS):
                    if isinstance(c, int) and c == 0 and i == 0:
                        pe.wait_ge(wl_ready, k + 1)
                    n = tile * HALF + k // 2
                    if k % 2 == 1:
                        bank, done = t_dve[(k // 2) % DRING], dve_bank
                        wait(pe, added, (n - DRING + 1) * HEADS)
                    else:
                        bank, done = t_act[(k // 2) % ARING], act_bank
                        wait(pe, weighed, n - ARING + 1)
                    w = slice(k * BANK, (k + 1) * BANK)
                    nc.tensor.matmul(bank[:, :], cur_hi[p][:, cols], w_hi[:, w], start=True, stop=False)
                    nc.tensor.matmul(bank[:, :], cur_hi[p][:, cols], w_lo[:, w], start=False, stop=False)
                    nc.tensor.matmul(bank[:, :], cur_lo[p][:, cols], w_hi[:, w], start=False, stop=True).then_inc(done, 1)

            def pooling(c, p):
                pe.wait_ge(cur2_ready, c + 1)
                pe.wait_ge(sel_ready, c + 1)
                first, last = isinstance(c, int) and c == 0, isinstance(c, int) and c == CHUNKS - 1
                nc.tensor.matmul(acc_pool2[:, :], sel[p][:, :], cur2_hi[p][:, :, :].rearrange("p i n -> p (i n)"),
                                 start=first, stop=False)
                nc.tensor.matmul(acc_pool2[:, :], sel[p][:, :], cur2_lo[p][:, :, :].rearrange("p i n -> p (i n)"),
                                 start=False, stop=last).then_inc(pool2_done, 1)

            pe.wait_ge(wh_ready, HEADS)
            pe.wait_ge(rows_written[0], 16 * 2)
            for _ in range(WARM_UPS):
                nc.tensor.matmul(acc1[:, :], w_hi[:, 0:128], w_hi[:, 0:BANK], start=True, stop=True)
            pe.wait_ge(v_ready, len(V_SUMS) + 4)
            layer1(0, 0, range(GROUPS + 1))

            def chunk(c, p):
                fixed = isinstance(c, int)
                more = not (fixed and c + 1 >= CHUNKS)
                layer2(c, 0, p)
                if more:
                    layer1(c + 1, 1 - p, range(0, 2))
                layer2(c, 1, p)
                if more:
                    layer1(c + 1, 1 - p, range(2, GROUPS + 1))
                layer2(c, 2, p)
                if not (fixed and c == 0):
                    pooling(c - 1, 1 - p)
                layer2(c, 3, p)

            over_chunks(pe, chunk)
            pe.wait_ge(top_loaded, 16 * 8)
            pe.wait_ge(pool1_ready, CHUNKS)
            for f in range(T1):
                pe.wait_ge(added, (CHUNKS * TILES * HALF - DRING + f + 1) * HEADS)
                rows = slice(f * 128, (f + 1) * 128)
                nc.tensor.matmul(t_dve[f][:, :], wt1_ctx[:, rows], ctx_sb[:, :], start=True, stop=False)
                nc.tensor.matmul(t_dve[f][:, :], wt1_sb[:, 0, rows], pool1[:, :, :].rearrange("n i x -> n (i x)"),
                                 start=False, stop=False)
            pooling(CHUNKS - 1, (CHUNKS - 1) % 2)
            pe.wait_ge(weighed, CHUNKS * TILES * HALF)
            pe.wait_ge(pool2_rows_ready, 1)
            for i in range(TILES):
                last = nc.tensor.transpose(t_act[0][:, i * 128:(i + 1) * 128], pool2_rows[:, i, :], ident[:, :])
            last.then_inc(pool2_turned, 1)
            pe.wait_ge(pool2_ready, 1)
            for f in range(T1):
                nc.tensor.matmul(t_dve[f][:, :], wt1_sb[:, 1, f * 128:(f + 1) * 128], pool2[:, :], start=False,
                                 stop=True).then_inc(top1_done, 1)
            for k in range(T1):
                pe.wait_ge(h1_ready, k + 1)
                for f in range(T2):
                    last = nc.tensor.matmul(t_act[f][:, :], wt2_sb[:, k, f * 128:(f + 1) * 128], h1[:, k, :],
                                            start=k == 0, stop=k == T1 - 1)
                    if k == T1 - 1:
                        last.then_inc(top2_done, 1)
            for k in range(T2):
                pe.wait_ge(h2_ready, k + 1)
                last = nc.tensor.matmul(acc1[0:1, :], wt3_sb[:, k:k + 1], h2[:, k, :], start=k == 0, stop=k == T2 - 1)
            last.then_inc(top3_done, 1)


def kernel(**inputs):
    import numpy as np
    import concourse.bacc as bacc
    from concourse import mybir
    from concourse.bass_utils import run_bass_kernel_spmd

    def host(name):
        return np.asarray(inputs[name])

    tables = [host(f"tbl_{f}") for f in range(FIELDS)]
    starts = np.concatenate([[0], np.cumsum([t.shape[0] for t in tables])[:-1]]).astype(np.int32)
    shift, field = np.arange(SHIFTS * GROUPS)[:, None], np.arange(FIELDS)[None, :]
    w0 = host("L0_rec_filter_0").reshape(FIELDS, FIELDS, MAPS)

    def by_group(a):
        return a.reshape(SHIFTS, GROUPS, FIELDS, MAPS).transpose(0, 2, 1, 3).reshape(128, GROUPS, MAPS)

    arrays = {
        "table": np.concatenate(tables),
        "ids": np.concatenate([host("ids").reshape(QUARTERS, ROWS, FIELDS).transpose(0, 2, 1).reshape(128, ROWS),
                               np.tile(starts, QUARTERS)[:, None]], axis=1),
        "dense": host("dense_ctx").reshape(QUARTERS, CHUNKS, TILES, CTX).transpose(3, 2, 1, 0).reshape(CTX, BATCH),
        "w0a": by_group(w0[field, (field + shift) % FIELDS]),
        "w0b": by_group(w0[(field + shift) % FIELDS, field]),
        "w0c": w0[np.arange(FIELDS), (np.arange(FIELDS) + FIELDS // 2) % FIELDS],
        "w1": host("L0_rec_filter_1").reshape(FIELDS, MAPS, MAPS).transpose(1, 0, 2).reshape(MAPS, FIELDS * MAPS),
        "wt1": host("W_top1"),
        "bt1": host("b_top1").reshape(T1, 128).T,
        "wt2": host("W_top2"),
        "bt2": host("b_top2").reshape(T2, 128).T,
        "wt3": host("W_top3").reshape(T2, 128).T,
        "select": np.pad(np.repeat(np.eye(QUARTERS, dtype=np.float32), DIM, axis=0),
                         ((0, 0), (128 - QUARTERS, 128 - QUARTERS))),
        "identity": np.eye(128, dtype=np.float32),
    }
    nc = bacc.Bacc("TRN2", target_bir_lowering=False, num_devices=1)
    given, args = {}, []
    for name, a in arrays.items():
        a = np.ascontiguousarray(a)
        given[f"{name}_dram"] = a
        args.append(nc.dram_tensor(f"{name}_dram", a.shape, mybir.dt.from_np(a.dtype), kind="ExternalInput").ap())
    args.append(nc.dram_tensor("y_dram", (1, BATCH), mybir.dt.float32, kind="ExternalOutput").ap())
    dlrm_tower(nc, *args)
    result = run_bass_kernel_spmd(nc, [given], core_ids=[0])
    y = result.results[0]["y_dram"]
    return y.reshape(TILES, CHUNKS, QUARTERS).transpose(2, 1, 0).reshape(BATCH, 1)
```

```python
from contextlib import ExitStack

import concourse.bass as bass
from concourse import mybir

FIELDS, DIM, BATCH = 32, 32, 512
MAPS = 128
QUARTERS = 128 // FIELDS
ROWS = BATCH // QUARTERS
TILES = 4
CHUNKS = ROWS // TILES
COLS = TILES * 128
RUN = TILES * DIM
SHIFTS = 4
GROUPS = 4
SPLIT = 2
WHOLE = GROUPS - SPLIT
BANK = 512
V_SUMS = [(slice(0, FIELDS), slice(1, GROUPS)), (slice(FIELDS, 2 * FIELDS), slice(0, GROUPS)),
          (slice(2 * FIELDS, 4 * FIELDS), slice(0, GROUPS))]
HEADS = BANK // MAPS
BANKS = FIELDS // HEADS
HALF = BANKS // 2
FEEDS = HALF * HEADS
DRING, ARING = 4, 2
SEL_WIDE = 2 * 128 - QUARTERS
CTX, TOP1, TOP2 = 16, 512, 256
T1, T2 = TOP1 // 128, TOP2 // 128
W_PIECES = BANKS
W_EARLY = 6
W_PIECE = FIELDS * MAPS // W_PIECES
FOLDS = [(slice(2, 9), slice(9, 16)), (slice(2, 5), slice(5, 8)), (slice(2, 4), slice(4, 9, 4))]
WARM_UPS = 14
HOLD_UPS = 8
TOP_PEEL = 4
LEAD = 3


def dlrm_tower(nc, table, ids, dense, w0a, w0b, w0c, w1, wt1, bt1, wt2, bt2, wt3, select, identity, out):
    fp32, f32r, i32 = mybir.dt.float32, mybir.dt.float32r, mybir.dt.int32
    ALU = mybir.AluOpType
    ACT = mybir.ActivationFunctionType
    AX = mybir.AxisListType

    with ExitStack() as ctx:
        def sb(name, shape, dt=fp32):
            return ctx.enter_context(nc.sbuf_tensor(name, shape, dt))

        def sem(name):
            return ctx.enter_context(nc.semaphore(name))

        x_rows = nc.dram_tensor("x_rows", (2, 2 * FIELDS, COLS), fp32, kind="Internal").ap()

        raw_ids = sb("raw_ids", [128, ROWS + 1], i32)
        all_ids = sb("all_ids", [128, ROWS], i32)
        row_ids = [sb(f"row_ids{p}", [128, TILES], i32) for p in range(2)]
        emb = [sb(f"emb{p}", [128, RUN]) for p in range(2)]
        weigh = [sb(f"weigh{p}", [128, TILES, FIELDS]) for p in range(2)]
        x_same = [sb(f"x_same{p}", [128, COLS]) for p in range(2)]
        x_shift = [sb(f"x_shift{p}", [128, GROUPS, COLS]) for p in range(2)]
        x_last = [sb(f"x_last{p}", [3 * FIELDS, COLS]) for p in range(2)]
        z = [sb(f"z{p}", [128, GROUPS, COLS]) for p in range(2)]
        z_last = [sb(f"z_last{p}", [3 * FIELDS, COLS]) for p in range(2)]
        z_hi = sb("z_hi", [128, SPLIT, COLS], f32r)
        z_lo = sb("z_lo", [128, SPLIT, COLS], f32r)
        z_parts = [sb(f"z_parts{p}", [3 * FIELDS, COLS], f32r) for p in range(2)]
        v = sb("v", [128, GROUPS, MAPS])
        v_b = sb("v_b", [128, GROUPS, MAPS])
        v_last = sb("v_last", [3 * FIELDS, MAPS])
        v_hi = sb("v_hi", [128, SPLIT, MAPS], f32r)
        v_lo = sb("v_lo", [128, SPLIT, MAPS], f32r)
        v_parts = sb("v_parts", [3 * FIELDS, MAPS], f32r)
        cur1 = [sb(f"cur1_{p}", [128, COLS]) for p in range(2)]
        cur_hi = [sb(f"cur_hi{p}", [128, COLS], f32r) for p in range(2)]
        cur_lo = [sb(f"cur_lo{p}", [128, COLS], f32r) for p in range(2)]
        w_raw = sb("w_raw", [128, FIELDS * MAPS])
        w_hi = sb("w_hi", [128, FIELDS * MAPS], f32r)
        w_lo = sb("w_lo", [128, FIELDS * MAPS], f32r)
        part = [sb(f"part{p}", [128, TILES, 2, MAPS]) for p in range(2)]
        prod = [sb(f"prod{i}", [128, FEEDS, MAPS]) for i in range(TILES)]
        side = [sb(f"side{p}", [128, TILES, MAPS]) for p in range(2)]
        whole = sb("whole", [128, TILES, MAPS])
        cur2_hi = [sb(f"cur2_hi{p}", [128, TILES, MAPS], f32r) for p in range(2)]
        cur2_lo = [sb(f"cur2_lo{p}", [128, TILES, MAPS], f32r) for p in range(2)]
        sel_wide = sb("sel_wide", [128, SEL_WIDE])
        sel = [sb(f"sel{p}", [128, 128], f32r) for p in range(2)]
        ident = sb("ident", [128, 128])
        pool1 = sb("pool1", [128, TILES, CHUNKS * QUARTERS])
        ctx_sb = sb("ctx_sb", [CTX, BATCH])
        wt1_ctx = sb("wt1_ctx", [CTX, TOP1])
        bt1_sb = sb("bt1_sb", [128, T1])
        bt2_sb = sb("bt2_sb", [128, T2])
        wt3_sb = sb("wt3_sb", [128, T2])
        wt1_hi, wt1_lo = sb("wt1_hi", [128, 2, TOP1], f32r), sb("wt1_lo", [128, 2, TOP1], f32r)
        wt2_hi, wt2_lo = sb("wt2_hi", [128, T1, TOP2], f32r), sb("wt2_lo", [128, T1, TOP2], f32r)
        wt1_raw = w_raw[:, 0:2 * TOP1].rearrange("p (k n) -> p k n", k=2)
        wt2_raw = w_raw[:, 2 * TOP1:2 * TOP1 + T1 * TOP2].rearrange("p (k n) -> p k n", k=T1)
        h2 = w_raw[:, 2 * TOP1 + T1 * TOP2:2 * TOP1 + T1 * TOP2 + T2 * BATCH].rearrange("n (f b) -> n f b", f=T2)
        pool1_hi, pool1_lo = z_hi[:, 0, :], z_lo[:, 0, :]
        pool2_rows = x_same[0].rearrange("x (i n) -> x i n", i=TILES)
        h1 = z[0]
        h1_hi, h1_lo = (w[:, 0:T1 * BATCH].rearrange("n (f b) -> n f b", f=T1) for w in (w_hi, w_lo))
        pool2_hi, pool2_lo = (w[:, T1 * BATCH:(T1 + 1) * BATCH] for w in (w_hi, w_lo))
        top_pieces = [(raw[:, k:k + BANK // n, :], hi[:, k:k + BANK // n, :], lo[:, k:k + BANK // n, :])
                      for raw, hi, lo, blocks, n in ((wt1_raw, wt1_hi, wt1_lo, 2, TOP1), (wt2_raw, wt2_hi, wt2_lo, T1, TOP2))
                      for k in range(0, blocks, BANK // n)]
        top_pieces.append((pool1[:, :, :].rearrange("n i x -> n (i x)"), pool1_hi, pool1_lo))
        y_sb = sb("y_sb", [1, BATCH])

        def ps(name):
            return ctx.enter_context(nc.psum_tensor(name, [128, BANK], fp32))

        t_dve = [ps(f"t_dve{r}") for r in range(DRING)]
        t_act = [ps(f"t_act{r}") for r in range(ARING)]
        acc1 = ps("acc1")
        acc_pool2 = ps("acc_pool2")

        ids_loaded, v_loaded, sel_loaded, top_loaded = (
            sem("ids_loaded"), sem("v_loaded"), sem("sel_loaded"), sem("top_loaded"))
        w_loaded = [sem(f"w_loaded{k}") for k in range(W_PIECES)]
        gathered = [sem(f"gathered{p}") for p in range(2)]
        rows_written = [sem(f"rows_written{p}") for p in range(2)]
        x_first = [sem(f"x_first{p}") for p in range(2)]
        x_rest = [sem(f"x_rest{p}") for p in range(2)]
        out_written = sem("out_written")
        ids_ready = sem("ids_ready")
        row_ids_ready = sem("row_ids_ready")
        v_ready, wh_ready, wl_ready = sem("v_ready"), sem("wh_ready"), sem("wl_ready")
        weigh_ready = sem("weigh_ready")
        z_ready = sem("z_ready")
        z_rounded = sem("z_rounded")
        pair_rounded = sem("pair_rounded")
        z_parts_ready = sem("z_parts_ready")
        z_lo_ready = sem("z_lo_ready")
        layer1_done = sem("layer1_done")
        hi_ready, cur1_ready = sem("hi_ready"), sem("cur1_ready")
        lo_ready = sem("lo_ready")
        pool1_ready = sem("pool1_ready")
        dve_bank, act_bank = sem("dve_bank"), sem("act_bank")
        added = sem("added")
        weighed = sem("weighed")
        folded = sem("folded")
        side_ready = sem("side_ready")
        summed = sem("summed")
        sel_ready = sem("sel_ready")
        cur2_hi_ready = sem("cur2_hi_ready")
        cur2_ready = sem("cur2_ready")
        pool2_done = sem("pool2_done")
        pool2_rows_ready = sem("pool2_rows_ready")
        pool2_turned = sem("pool2_turned")
        pool2_hi_ready, pool2_lo_ready = sem("pool2_hi_ready"), sem("pool2_lo_ready")
        top_hi_ready, top_lo_ready = sem("top_hi_ready"), sem("top_lo_ready")
        last_side_ready = sem("last_side_ready")
        h1_hi_ready = sem("h1_hi_ready")
        h1_own = sem("h1_own")
        h1_given = sem("h1_given")
        h1_lo_ready = sem("h1_lo_ready")
        top1_done, top2_done, top3_done = sem("top1_done"), sem("top2_done"), sem("top3_done")
        h2_ready, y_ready = sem("h2_ready"), sem("y_ready")

        block = ctx.enter_context(nc.Block())

        def wait(eng, s, value):
            if not (isinstance(value, int) and value <= 0):
                eng.wait_ge(s, value)

        def over_chunks(eng, chunk, head=2, tail=2, after_head=None):
            for c in range(head):
                chunk(c, c % 2)
            if after_head is not None:
                after_head()
            with eng.Fori(head // 2, (CHUNKS - tail) // 2) as pair:
                for parity in range(2):
                    chunk(pair * 2 + parity, parity)
            for c in range(CHUNKS - tail, CHUNKS):
                chunk(c, c % 2)

        def before(c, parity):
            return (c - parity) // 2

        @block.sync
        def _(sp):
            sp.dma_start(raw_ids[:, :], ids).then_inc(ids_loaded, 16)

            def chunk(c, p):
                turn = before(c, p) + 1
                wait(sp, layer1_done, c - 1)
                sp.wait_ge(gathered[p], turn * (16 * TILES))
                rows = x_rows[p].rearrange("h (q c) -> q h c", q=QUARTERS)
                sp.dma_start(rows[:, 0:FIELDS], emb[p][:, :]).then_inc(rows_written[p], 16)
                sp.dma_start(rows[:, FIELDS:2 * FIELDS], emb[p][:, :]).then_inc(rows_written[p], 16)
                sp.wait_ge(rows_written[p], turn * (16 * 2))
                src = x_rows[p]
                first, stride = src.offset, COLS

                def shifted(first_group, groups):
                    return bass.AP(src.tensor, first + first_group * stride,
                                   [[GROUPS * stride, SHIFTS], [stride, FIELDS], [1, groups * COLS]])

                sp.dma_start(x_same[p][:, :],
                             bass.AP(src.tensor, first, [[0, SHIFTS], [stride, FIELDS], [1, COLS]])).then_inc(x_first[p], 16)
                sp.dma_start(x_shift[p][:, 0:WHOLE, :].rearrange("p g c -> p (g c)"),
                             shifted(0, WHOLE)).then_inc(x_first[p], 16)
                sp.dma_start(x_last[p][:, :],
                             bass.AP(src.tensor, first + FIELDS // 2 * stride,
                                     [[0, 3], [stride, FIELDS], [1, COLS]])).then_inc(x_rest[p], 16)
                sp.dma_start(x_shift[p][:, WHOLE:GROUPS, :].rearrange("p g c -> p (g c)"),
                             shifted(WHOLE, SPLIT)).then_inc(x_rest[p], 16)

            def top_loads():
                sp.wait_ge(wl_ready, W_PIECES)
                sp.dma_start(ctx_sb[:, :], dense).then_inc(top_loaded, 16)
                sp.dma_start(ident[:, :], identity).then_inc(top_loaded, 16)
                sp.dma_start(wt1_raw, wt1[0:256, :].rearrange("(k p) n -> p k n", p=128)).then_inc(top_loaded, 16)
                sp.dma_start(wt1_ctx[:, :], wt1[256:256 + CTX, :]).then_inc(top_loaded, 16)
                sp.dma_start(bt1_sb[:, :], bt1).then_inc(top_loaded, 16)
                sp.dma_start(wt2_raw, wt2.rearrange("(k p) n -> p k n", p=128)).then_inc(top_loaded, 16)
                sp.dma_start(bt2_sb[:, :], bt2).then_inc(top_loaded, 16)
                sp.dma_start(wt3_sb[:, :], wt3).then_inc(top_loaded, 16)

            over_chunks(sp, chunk, after_head=top_loads)
            sp.wait_ge(y_ready, 1)
            sp.dma_start(out, y_sb[:, :]).then_inc(out_written, 16)
            sp.wait_ge(out_written, 16)

        @block.gpsimd
        def _(pool):
            def stage(c, p):
                wait(pool, rows_written[p], before(c, p) * (16 * 2))
                wait(pool, weigh_ready, c - 1)
                nc.gpsimd.tensor_copy(row_ids[p][:, :], all_ids[:, bass.ds(c * TILES, TILES)]).then_inc(row_ids_ready, 1)

            def gather(p, which):
                for i in which:
                    nc.gpsimd.indirect_dma_start(
                        emb[p][:, i * DIM:(i + 1) * DIM], None, table,
                        bass.IndirectOffsetOnAxis(ap=row_ids[p][:, i:i + 1], axis=0)).then_inc(gathered[p], 16)

            def lower_last(c, p):
                low = slice(0, FIELDS)
                pool.wait_ge(z_rounded, c)
                nc.gpsimd.tensor_tensor(z_parts[p][low, :], z_last[p][low, :], z_parts[p][low, :].bitcast(fp32),
                                        ALU.subtract).then_inc(z_parts_ready, 1)

            def lower_pair(c, p):
                pool.wait_ge(pair_rounded, c)
                pool.wait_ge(layer1_done, c)
                nc.gpsimd.tensor_tensor(z_lo[:, 0, :], z[p][:, WHOLE, :], z_hi[:, 0, :].bitcast(fp32),
                                        ALU.subtract).then_inc(z_parts_ready, 1)

            def fold(c, i, p, staged=None):
                src = prod[i]
                tile = c * TILES + i
                pool.wait_ge(weighed, (tile + 1) * HALF)
                for step, (dst, other) in enumerate(FOLDS):
                    if step > 0:
                        pool.wait_ge(folded, tile * len(FOLDS) + step)
                    nc.gpsimd.tensor_tensor(src[:, dst, :], src[:, dst, :], src[:, other, :], ALU.add).then_inc(folded, 1)
                pool.wait_ge(folded, (tile + 1) * len(FOLDS))
                if i == 0:
                    wait(pool, summed, (c - 1) * 2)
                if staged is not None:
                    pool.wait_ge(row_ids_ready, staged + 1)
                nc.gpsimd.tensor_tensor(side[p][:, i, :], src[:, 2, :], src[:, 3, :], ALU.add).then_inc(side_ready, 1)

            def lower_top(n):
                raw, hi, lo = top_pieces[n]
                pool.wait_ge(top_hi_ready, n + 1)
                nc.gpsimd.tensor_tensor(lo, raw, hi.bitcast(fp32), ALU.subtract).then_inc(top_lo_ready, 1)

            pool.wait_ge(ids_ready, 1)
            for c in range(LEAD):
                stage(c, c % 2)
                pool.wait_ge(row_ids_ready, c + 1)
                gather(c % 2, range(TILES))
            lower_last(1, 1)

            def chunk(c, p):
                ahead = not (isinstance(c, int) and c + LEAD >= CHUNKS)
                if not (isinstance(c, int) and c + 1 >= CHUNKS):
                    lower_pair(c + 1, 1 - p)
                for i in range(TILES):
                    if isinstance(c, int) and c * TILES + i == CHUNKS * TILES - 1:
                        break
                    if ahead and i == 0:
                        stage(c + LEAD, (p + LEAD) % 2)
                    fold(c, i, p, staged=c + LEAD if ahead and i == 0 else None)
                    if ahead:
                        gather((p + LEAD) % 2, ((0,), (1,), (2, 3), ())[i])
                    if not ahead and i % 2 == 1:
                        n = (c - (CHUNKS - LEAD)) * 2 + i // 2
                        if n < len(top_pieces):
                            lower_top(n)
                if not (isinstance(c, int) and c + 2 >= CHUNKS):
                    lower_last(c + 2, p)

            over_chunks(pool, chunk, tail=4)

        @block.scalar
        def _(act):
            act.dma_start(v[:, :, :], w0a).then_inc(v_loaded, 16)
            act.dma_start(v_b[:, :, :], w0b).then_inc(v_loaded, 16)
            act.dma_start(v_last[:, :], bass.AP(w0c.tensor, w0c.offset, [[0, 3], [MAPS, FIELDS], [1, MAPS]])
                          ).then_inc(v_loaded, 16)

            def load_w(k):
                w = slice(k * W_PIECE, (k + 1) * W_PIECE)
                act.dma_start(w_raw[:, w], w1[:, w]).then_inc(w_loaded[k], 16)

            def upper_w(k):
                w = slice(k * W_PIECE, (k + 1) * W_PIECE)
                act.wait_ge(w_loaded[k], 16)
                nc.scalar.activation(w_hi[:, w], w_raw[:, w], ACT.Copy).then_inc(wh_ready, 1)

            def relu1(c, p):
                act.wait_ge(layer1_done, c + 1)
                wait(act, act_bank, (c - 1) * (TILES * HALF))
                nc.scalar.activation(cur_hi[p][:, :].rearrange("m (i q d) -> m i q d", i=TILES, q=QUARTERS),
                                     acc1[:, :].rearrange("m (q i d) -> m i q d", i=TILES, q=QUARTERS),
                                     ACT.Relu).then_inc(hi_ready, 1)
                wait(act, pool1_ready, c - 1)
                nc.scalar.activation(cur1[p][:, :], acc1[:, :], ACT.Relu).then_inc(cur1_ready, 1)

            def round_last(c, p):
                act.wait_ge(z_ready, c * 3 + 2)
                wait(act, layer1_done, c - 1)
                nc.scalar.activation(z_parts[p][:, :], z_last[p][:, :], ACT.Copy).then_inc(z_rounded, 1)

            def round_pair(c, p):
                act.wait_ge(z_ready, c * 3 + 3)
                act.wait_ge(layer1_done, c)
                nc.scalar.activation(z_hi[:, :, :], z[p][:, WHOLE:GROUPS, :], ACT.Copy).then_inc(pair_rounded, 1)

            def relu2(c, p):
                act.wait_ge(summed, c * 2 + 2)
                wait(act, pool2_done, c - 1)
                nc.scalar.activation(cur2_hi[p][:, :, :], whole[:, :, :], ACT.Relu).then_inc(cur2_hi_ready, 1)

            def weigh_tile(c, i, p):
                tile = c * TILES + i
                wait(act, side_ready, tile - TILES + 1)
                wait(act, added, (tile - TILES) * FEEDS + 2)
                if i == 0:
                    act.wait_ge(weigh_ready, c + 1)
                for k in range(HALF):
                    act.wait_ge(act_bank, tile * HALF + k + 1)
                    for j in range(HEADS):
                        h = HEADS * 2 * k + j
                        last = nc.scalar.activation(prod[i][:, HEADS * k + j, :],
                                                    t_act[k % ARING][:, j * MAPS:(j + 1) * MAPS], ACT.Copy,
                                                    scale=weigh[p][:, i, h:h + 1])
                    last.then_inc(weighed, 1)

            def upper_top(n):
                raw, hi, lo = top_pieces[n]
                if n == 0:
                    act.wait_ge(top_loaded, 16 * 8)
                if n == len(top_pieces) - 1:
                    act.wait_ge(pool1_ready, CHUNKS)
                    act.wait_ge(layer1_done, CHUNKS)
                nc.scalar.activation(hi, raw, ACT.Copy).then_inc(top_hi_ready, 1)

            def chunk(c, p):
                for i in range(TILES):
                    weigh_tile(c, i, p)
                    if i == 2 and isinstance(c, int) and c == CHUNKS - 1:
                        upper_top(len(top_pieces) - 1)
                    if i == 0 and isinstance(c, int) and c == 0:
                        round_last(1, 1)
                    if i == 0 and not (isinstance(c, int) and c + 1 >= CHUNKS):
                        round_pair(c + 1, 1 - p)
                    if i == 0 and isinstance(c, int) and 0 <= c - (CHUNKS - TOP_PEEL) < len(top_pieces) - 1:
                        upper_top(c - (CHUNKS - TOP_PEEL))
                    if i == 1 and not (isinstance(c, int) and c == 0):
                        relu2(c - 1, 1 - p)
                    if i == 1 and not (isinstance(c, int) and c + 1 >= CHUNKS):
                        relu1(c + 1, 1 - p)
                    if i == 2 and not (isinstance(c, int) and c + 2 >= CHUNKS):
                        round_last(c + 2, p)

            for k in range(W_EARLY):
                load_w(k)
            for k in range(W_EARLY):
                upper_w(k)
            act.wait_ge(x_rest[0], 16 * 2)
            for k in range(W_EARLY, W_PIECES):
                load_w(k)
            act.dma_start(sel_wide[:, :], select).then_inc(sel_loaded, 16)
            upper_w(W_EARLY)
            relu1(0, 0)
            for k in range(W_EARLY + 1, W_PIECES):
                upper_w(k)
            over_chunks(act, chunk, tail=TOP_PEEL)
            relu2(CHUNKS - 1, (CHUNKS - 1) % 2)

            act.wait_ge(pool2_turned, 1)
            nc.scalar.activation(pool2_hi, t_act[0][:, :], ACT.Copy).then_inc(pool2_hi_ready, 1)
            act.wait_ge(top_loaded, 16 * 8)
            for f in range(T1):
                act.wait_ge(top1_done, f + 1)
                nc.scalar.activation(h1_hi[:, f, :], t_dve[f][:, :], ACT.Relu, bias=bt1_sb[:, f:f + 1]).then_inc(h1_hi_ready, 1)
            for f in range(T1 // 2, T1):
                nc.scalar.activation(h1[:, f, :], t_dve[f][:, :], ACT.Relu, bias=bt1_sb[:, f:f + 1]).then_inc(h1_given, 1)
            for f in range(T2):
                act.wait_ge(top2_done, f + 1)
                nc.scalar.activation(h2[:, f, :], t_act[f][:, :], ACT.Relu, bias=bt2_sb[:, f:f + 1]).then_inc(h2_ready, 1)
            act.wait_ge(top3_done, 1)
            nc.scalar.activation(y_sb[:, :], acc1[0:1, :], ACT.Copy).then_inc(y_ready, 1)

        @block.vector
        def _(dve):
            dve.wait_ge(ids_loaded, 16)
            nc.vector.tensor_tensor(all_ids[:, :], raw_ids[:, 0:ROWS], raw_ids[:, ROWS:ROWS + 1].to_broadcast([128, ROWS]),
                                    ALU.add).then_inc(ids_ready, 1)

            def transpose(c, p):
                dve.wait_ge(gathered[p], (before(c, p) + 1) * (16 * TILES))
                wait(dve, weighed, (c - 1) * (TILES * HALF))
                wait(dve, added, (c - 1) * (TILES * FEEDS))
                nc.vector.transpose(weigh[p][:, :, :].rearrange("p i h -> p (i h)"), emb[p][:, :]).then_inc(weigh_ready, 1)

            def products(c, p, which):
                turn = before(c, p) + 1
                if which == 0:
                    dve.wait_ge(x_first[p], turn * (16 * 2))
                    wait(dve, layer1_done, c - 1)
                elif which == 2:
                    dve.wait_ge(x_rest[p], turn * (16 * 2))
                if which < 2:
                    g = slice(which * 2, which * 2 + 2)
                    nc.vector.tensor_tensor(z[p][:, g, :], x_shift[p][:, g, :],
                                            x_same[p][:, None, :].to_broadcast([128, 2, COLS]),
                                            ALU.mult).then_inc(z_ready, 1)
                else:
                    nc.vector.tensor_tensor(z_last[p][:, :], x_last[p][:, :], x_same[p][0:3 * FIELDS, :],
                                            ALU.mult).then_inc(z_ready, 1)

            def lower_pair(c, p):
                dve.wait_ge(pair_rounded, c)
                dve.wait_ge(layer1_done, c)
                nc.vector.tensor_tensor(z_lo[:, 1, :], z[p][:, WHOLE + 1, :], z_hi[:, 1, :].bitcast(fp32),
                                        ALU.subtract).then_inc(z_lo_ready, 1)

            def lower(c, p):
                dve.wait_ge(cur1_ready, c + 1)
                wait(dve, act_bank, (c - 1) * (TILES * HALF))
                nc.vector.tensor_tensor(
                    cur_lo[p][:, :].rearrange("m (i q d) -> m i q d", i=TILES, q=QUARTERS),
                    cur1[p][:, :].rearrange("m (q i d) -> m i q d", i=TILES, q=QUARTERS),
                    cur_hi[p][:, :].bitcast(fp32).rearrange("m (i q d) -> m i q d", i=TILES, q=QUARTERS),
                    ALU.subtract).then_inc(lo_ready, 1)

            def pooling1(c, p):
                dst = pool1[:, :, bass.ds(c * QUARTERS, QUARTERS)]
                nc.vector.tensor_reduce(dst.rearrange("m i q -> m q i"),
                                        cur1[p][:, :].rearrange("m (q i d) -> m q i d", i=TILES, q=QUARTERS),
                                        AX.X, ALU.add).then_inc(pool1_ready, 1)

            def add_tile(c, i, p):
                tile = c * TILES + i
                if i == 0:
                    wait(dve, summed, (c - 1) * 2)
                    dve.wait_ge(weigh_ready, c + 1)
                for k in range(HALF):
                    dve.wait_ge(dve_bank, tile * HALF + k + 1)
                    for j in range(HEADS):
                        h, step = HEADS * (2 * k + 1) + j, HEADS * k + j
                        src = t_dve[k % DRING][:, j * MAPS:(j + 1) * MAPS]
                        dst = part[p][:, i, step % 2, :]
                        w = weigh[p][:, i, h:h + 1]
                        if step < 2:
                            if step == 0:
                                dve.wait_ge(weighed, tile * HALF + 1)
                            nc.vector.scalar_tensor_tensor(dst, src, w, prod[i][:, step, :],
                                                           ALU.mult, ALU.add).then_inc(added, 1)
                        else:
                            dve.wait_ge(added, tile * FEEDS + step - 1)
                            nc.vector.scalar_tensor_tensor(dst, src, w, dst, ALU.mult, ALU.add).then_inc(added, 1)

            def last_side(p):
                dve.wait_ge(weighed, CHUNKS * TILES * HALF)
                nc.vector.tensor_reduce(side[p][:, TILES - 1, :], prod[TILES - 1][:, 2:FEEDS, :].rearrange("x h n -> x n h"),
                                        AX.X, ALU.add).then_inc(last_side_ready, 1)

            def finish(c, p):
                dve.wait_ge(added, (c + 1) * (TILES * FEEDS))
                wait(dve, cur2_hi_ready, c)
                wait(dve, cur2_ready, c)
                nc.vector.tensor_tensor(whole[:, :, :], part[p][:, :, 0, :], part[p][:, :, 1, :], ALU.add).then_inc(summed, 1)
                if isinstance(c, int) and c == CHUNKS - 1:
                    dve.wait_ge(side_ready, CHUNKS * TILES - 1)
                    last_side(p)
                    dve.wait_ge(last_side_ready, 1)
                else:
                    dve.wait_ge(side_ready, (c + 1) * TILES)
                dve.wait_ge(summed, c * 2 + 1)
                nc.vector.tensor_tensor(whole[:, :, :], whole[:, :, :], side[p][:, :, :], ALU.add).then_inc(summed, 1)

            def lower2(c, p):
                dve.wait_ge(summed, c * 2 + 2)
                dve.wait_ge(cur2_hi_ready, c + 1)
                wait(dve, pool2_done, c - 1)
                nc.vector.scalar_tensor_tensor(cur2_lo[p][:, :, :], whole[:, :, :], 0.0,
                                               cur2_hi[p][:, :, :].bitcast(fp32), ALU.max,
                                               ALU.subtract).then_inc(cur2_ready, 1)

            def place(c, p):
                wait(dve, pool2_done, c - 1)
                nc.vector.tensor_copy(sel[p][:, :], sel_wide[:, bass.ds(c * -QUARTERS + (CHUNKS - 1) * QUARTERS, 128)]
                                      ).then_inc(sel_ready, 1)

            dve.wait_ge(v_loaded, 48)
            for rows, groups in V_SUMS:
                nc.vector.tensor_tensor(v[rows, groups, :], v[rows, groups, :], v_b[rows, groups, :],
                                        ALU.add).then_inc(v_ready, 1)
            nc.vector.tensor_copy(v_parts[:, :], v_last[:, :]).then_inc(v_ready, 1)
            low = slice(2 * FIELDS, 3 * FIELDS)
            dve.wait_ge(v_ready, len(V_SUMS) + 1)
            nc.vector.tensor_tensor(v_parts[low, :], v_last[low, :], v_parts[low, :].bitcast(fp32),
                                    ALU.subtract).then_inc(v_ready, 1)
            nc.vector.tensor_copy(v_hi[:, :, :], v[:, WHOLE:GROUPS, :]).then_inc(v_ready, 1)
            dve.wait_ge(v_ready, len(V_SUMS) + 3)
            nc.vector.tensor_tensor(v_lo[:, :, :], v[:, WHOLE:GROUPS, :], v_hi[:, :, :].bitcast(fp32),
                                    ALU.subtract).then_inc(v_ready, 1)
            transpose(0, 0)

            def lower_w(k):
                w = slice(k * W_PIECE, (k + 1) * W_PIECE)
                dve.wait_ge(wh_ready, k + 1)
                nc.vector.tensor_tensor(w_lo[:, w], w_raw[:, w], w_hi[:, w].bitcast(fp32), ALU.subtract).then_inc(wl_ready, 1)

            for k in range(W_EARLY):
                lower_w(k)
            for which in (0, 2, 1):
                products(0, 0, which)
            lower_w(W_EARLY)
            lower(0, 0)
            for k in range(W_EARLY + 1, W_PIECES):
                lower_w(k)
            pooling1(0, 0)
            for which in (0, 2, 1):
                products(1, 1, which)

            def chunk(c, p):
                fixed = isinstance(c, int)
                more1, more2 = not (fixed and c + 1 >= CHUNKS), not (fixed and c + 2 >= CHUNKS)
                if more1:
                    transpose(c + 1, 1 - p)
                add_tile(c, 0, p)
                if more1:
                    lower_pair(c + 1, 1 - p)
                if not (fixed and c == 0):
                    finish(c - 1, 1 - p)
                add_tile(c, 1, p)
                if not (fixed and c == 0):
                    lower2(c - 1, 1 - p)
                if more2:
                    products(c + 2, p, 0)
                    products(c + 2, p, 2)
                add_tile(c, 2, p)
                if more1:
                    lower(c + 1, 1 - p)
                    pooling1(c + 1, 1 - p)
                place(c, p)
                add_tile(c, 3, p)
                if more2:
                    products(c + 2, p, 1)

            dve.wait_ge(sel_loaded, 16)
            over_chunks(dve, chunk)
            finish(CHUNKS - 1, (CHUNKS - 1) % 2)
            lower2(CHUNKS - 1, (CHUNKS - 1) % 2)
            dve.wait_ge(pool2_done, CHUNKS)
            nc.vector.tensor_copy(pool2_rows.rearrange("x i n -> x (i n)"), acc_pool2[:, :]).then_inc(pool2_rows_ready, 1)
            dve.wait_ge(pool2_turned, 1)
            dve.wait_ge(pool2_hi_ready, 1)
            nc.vector.tensor_tensor(pool2_lo, t_act[0][:, :], pool2_hi.bitcast(fp32), ALU.subtract).then_inc(pool2_lo_ready, 1)
            dve.wait_ge(top_loaded, 16 * 8)
            for f in range(T1):
                dve.wait_ge(h1_hi_ready, f + 1)
                if f < T1 // 2:
                    nc.vector.tensor_scalar(h1[:, f, :], t_dve[f][:, :], bt1_sb[:, f:f + 1], 0.0, ALU.add, ALU.max
                                            ).then_inc(h1_own, 1)
                    dve.wait_ge(h1_own, f + 1)
                else:
                    dve.wait_ge(h1_given, f - T1 // 2 + 1)
                nc.vector.tensor_tensor(h1_lo[:, f, :], h1[:, f, :], h1_hi[:, f, :].bitcast(fp32), ALU.subtract
                                        ).then_inc(h1_lo_ready, 1)

        @block.tensor
        def _(pe):
            def first_layer1():
                low = slice(0, FIELDS)
                for which, operands in enumerate(([(v[:, g, :], z[0][:, g, :]) for g in range(WHOLE)],
                                                  [(v_last[low, :], z_last[0][low, :])],
                                                  [(v[:, g, :], z[0][:, g, :]) for g in range(WHOLE, GROUPS)])):
                    pe.wait_ge(z_ready, which + 1)
                    for k, (weights, rows) in enumerate(operands):
                        last = nc.tensor.matmul(acc1[:, :], weights, rows, start=which == 0 and k == 0,
                                                stop=which == 2 and k == SPLIT - 1)
                last.then_inc(layer1_done, 1)

            def layer1(c, p, groups):
                if groups[0] == 0:
                    pe.wait_ge(lo_ready, c)
                    pe.wait_ge(cur1_ready, c)
                for g in groups:
                    if g < WHOLE:
                        if g == 0:
                            pe.wait_ge(z_ready, c * 3 + 1)
                        nc.tensor.matmul(acc1[:, :], v[:, g, :], z[p][:, g, :], start=g == 0, stop=False)
                    elif g < GROUPS:
                        k = g - WHOLE
                        if k == 0:
                            pe.wait_ge(z_parts_ready, c * 2)
                        else:
                            pe.wait_ge(z_lo_ready, c)
                        nc.tensor.matmul(acc1[:, :], v_hi[:, k, :], z_hi[:, k, :], start=False, stop=False)
                        nc.tensor.matmul(acc1[:, :], v_lo[:, k, :], z_hi[:, k, :], start=False, stop=False)
                        nc.tensor.matmul(acc1[:, :], v_hi[:, k, :], z_lo[:, k, :], start=False, stop=False)
                    else:
                        nc.tensor.matmul(acc1[:, :], v_parts[:, :], z_parts[p][:, :], start=False,
                                         stop=True).then_inc(layer1_done, 1)

            def layer2(c, i, p):
                tile = c * TILES + i
                cols = slice(i * 128, (i + 1) * 128)
                if i == 0:
                    pe.wait_ge(hi_ready, c + 1)
                    pe.wait_ge(lo_ready, c + 1)
                for k in range(BANKS):
                    if isinstance(c, int) and c == 0 and i == 0:
                        pe.wait_ge(wl_ready, k + 1)
                    n = tile * HALF + k // 2
                    if k % 2 == 1:
                        bank, done = t_dve[(k // 2) % DRING], dve_bank
                        wait(pe, added, (n - DRING + 1) * HEADS)
                    else:
                        bank, done = t_act[(k // 2) % ARING], act_bank
                        wait(pe, weighed, n - ARING + 1)
                    w = slice(k * BANK, (k + 1) * BANK)
                    nc.tensor.matmul(bank[:, :], cur_hi[p][:, cols], w_hi[:, w], start=True, stop=False)
                    nc.tensor.matmul(bank[:, :], cur_hi[p][:, cols], w_lo[:, w], start=False, stop=False)
                    nc.tensor.matmul(bank[:, :], cur_lo[p][:, cols], w_hi[:, w], start=False, stop=True).then_inc(done, 1)

            def pooling(c, p):
                pe.wait_ge(cur2_ready, c + 1)
                pe.wait_ge(sel_ready, c + 1)
                first, last = isinstance(c, int) and c == 0, isinstance(c, int) and c == CHUNKS - 1
                nc.tensor.matmul(acc_pool2[:, :], sel[p][:, :], cur2_hi[p][:, :, :].rearrange("p i n -> p (i n)"),
                                 start=first, stop=False)
                nc.tensor.matmul(acc_pool2[:, :], sel[p][:, :], cur2_lo[p][:, :, :].rearrange("p i n -> p (i n)"),
                                 start=False, stop=last).then_inc(pool2_done, 1)

            def warm_up(times, bank):
                for _ in range(times):
                    nc.tensor.matmul(bank[:, :], w_hi[:, 0:128], w_hi[:, 0:BANK], start=True, stop=True)

            def top_ctx(f):
                nc.tensor.matmul(t_dve[f][:, :], wt1_ctx[:, f * 128:(f + 1) * 128], ctx_sb[:, :], start=False, stop=False)

            pe.wait_ge(wh_ready, HEADS)
            pe.wait_ge(rows_written[0], 16 * 2)
            warm_up(WARM_UPS, t_dve[DRING - 1])
            pe.wait_ge(v_ready, len(V_SUMS) + 4)
            first_layer1()
            warm_up(HOLD_UPS, t_dve[DRING - 1])

            def chunk(c, p):
                fixed = isinstance(c, int)
                more = not (fixed and c + 1 >= CHUNKS)
                layer2(c, 0, p)
                if more:
                    layer1(c + 1, 1 - p, range(0, 2))
                layer2(c, 1, p)
                if more:
                    layer1(c + 1, 1 - p, range(2, GROUPS + 1))
                layer2(c, 2, p)
                if not (fixed and c == 0):
                    pooling(c - 1, 1 - p)
                layer2(c, 3, p)

            over_chunks(pe, chunk)
            pe.wait_ge(top_loaded, 16 * 8)
            pe.wait_ge(top_lo_ready, len(top_pieces))
            for f in range(T1):
                pe.wait_ge(added, (CHUNKS * TILES * HALF - DRING + f + 1) * HEADS)
                rows = slice(f * 128, (f + 1) * 128)
                for w, x in ((wt1_hi, pool1_hi), (wt1_lo, pool1_hi), (wt1_hi, pool1_lo)):
                    nc.tensor.matmul(t_dve[f][:, :], w[:, 0, rows], x, start=w is wt1_hi and x is pool1_hi, stop=False)
            top_ctx(0)
            top_ctx(1)
            warm_up(HOLD_UPS, acc1)
            pooling(CHUNKS - 1, (CHUNKS - 1) % 2)
            top_ctx(2)
            pe.wait_ge(weighed, CHUNKS * TILES * HALF)
            pe.wait_ge(pool2_rows_ready, 1)
            for i in range(TILES):
                last = nc.tensor.transpose(t_act[0][:, i * 128:(i + 1) * 128], pool2_rows[:, i, :], ident[:, :])
            last.then_inc(pool2_turned, 1)
            top_ctx(3)

            def pool2_upper(f):
                for w in (wt1_hi, wt1_lo):
                    nc.tensor.matmul(t_dve[f][:, :], w[:, 1, f * 128:(f + 1) * 128], pool2_hi, start=False, stop=False)

            def h1_upper(k):
                pe.wait_ge(h1_hi_ready, k + 1)
                for f in range(T2):
                    for w in (wt2_hi, wt2_lo):
                        nc.tensor.matmul(t_act[f][:, :], w[:, k, f * 128:(f + 1) * 128], h1_hi[:, k, :],
                                         start=k == 0 and w is wt2_hi, stop=False)

            pe.wait_ge(pool2_hi_ready, 1)
            for f in range(T1 - 1):
                pool2_upper(f)
            pe.wait_ge(pool2_lo_ready, 1)
            for f in range(T1):
                nc.tensor.matmul(t_dve[f][:, :], wt1_hi[:, 1, f * 128:(f + 1) * 128], pool2_lo, start=False,
                                 stop=True).then_inc(top1_done, 1)
                if f == 0:
                    pool2_upper(T1 - 1)
            h1_upper(0)
            for k in range(T1):
                if k + 1 < T1:
                    h1_upper(k + 1)
                pe.wait_ge(h1_lo_ready, k + 1)
                for f in range(T2):
                    last = nc.tensor.matmul(t_act[f][:, :], wt2_hi[:, k, f * 128:(f + 1) * 128], h1_lo[:, k, :],
                                            start=False, stop=k == T1 - 1)
                    if k == T1 - 1:
                        last.then_inc(top2_done, 1)
            for k in range(T2):
                pe.wait_ge(h2_ready, k + 1)
                last = nc.tensor.matmul(acc1[0:1, :], wt3_sb[:, k:k + 1], h2[:, k, :], start=k == 0, stop=k == T2 - 1)
            last.then_inc(top3_done, 1)


def kernel(**inputs):
    import numpy as np
    import concourse.bacc as bacc
    from concourse import mybir
    from concourse.bass_utils import run_bass_kernel_spmd

    def host(name):
        return np.asarray(inputs[name])

    tables = [host(f"tbl_{f}") for f in range(FIELDS)]
    starts = np.concatenate([[0], np.cumsum([t.shape[0] for t in tables])[:-1]]).astype(np.int32)
    shift, field = np.arange(SHIFTS * GROUPS)[:, None], np.arange(FIELDS)[None, :]
    w0 = host("L0_rec_filter_0").reshape(FIELDS, FIELDS, MAPS)

    def by_group(a):
        return a.reshape(SHIFTS, GROUPS, FIELDS, MAPS).transpose(0, 2, 1, 3).reshape(128, GROUPS, MAPS)

    arrays = {
        "table": np.concatenate(tables),
        "ids": np.concatenate([host("ids").reshape(QUARTERS, ROWS, FIELDS).transpose(0, 2, 1).reshape(128, ROWS),
                               np.tile(starts, QUARTERS)[:, None]], axis=1),
        "dense": host("dense_ctx").reshape(QUARTERS, CHUNKS, TILES, CTX).transpose(3, 2, 1, 0).reshape(CTX, BATCH),
        "w0a": by_group(w0[field, (field + shift) % FIELDS]),
        "w0b": by_group(w0[(field + shift) % FIELDS, field]),
        "w0c": w0[np.arange(FIELDS), (np.arange(FIELDS) + FIELDS // 2) % FIELDS],
        "w1": host("L0_rec_filter_1").reshape(FIELDS, MAPS, MAPS).transpose(1, 0, 2).reshape(MAPS, FIELDS * MAPS),
        "wt1": host("W_top1"),
        "bt1": host("b_top1").reshape(T1, 128).T,
        "wt2": host("W_top2"),
        "bt2": host("b_top2").reshape(T2, 128).T,
        "wt3": host("W_top3").reshape(T2, 128).T,
        "select": np.pad(np.repeat(np.eye(QUARTERS, dtype=np.float32), DIM, axis=0),
                         ((0, 0), (128 - QUARTERS, 128 - QUARTERS))),
        "identity": np.eye(128, dtype=np.float32),
    }
    nc = bacc.Bacc("TRN2", target_bir_lowering=False, num_devices=1)
    given, args = {}, []
    for name, a in arrays.items():
        a = np.ascontiguousarray(a)
        given[f"{name}_dram"] = a
        args.append(nc.dram_tensor(f"{name}_dram", a.shape, mybir.dt.from_np(a.dtype), kind="ExternalInput").ap())
    args.append(nc.dram_tensor("y_dram", (1, BATCH), mybir.dt.float32, kind="ExternalOutput").ap())
    dlrm_tower(nc, *args)
    result = run_bass_kernel_spmd(nc, [given], core_ids=[0])
    y = result.results[0]["y_dram"]
    return y.reshape(TILES, CHUNKS, QUARTERS).transpose(2, 1, 0).reshape(BATCH, 1)
```
